# Optimizing a Trainium2 kernel written in Bass

```python
import numpy as np
import jax
import jax.numpy as jnp

def _softmax(x, axis=-1):
    return jax.nn.softmax(x, axis=axis)

def _gelu(x):
    return jax.nn.gelu(x, approximate=True)

def _silu(x):
    return jax.nn.silu(x)

def _sigmoid(x):
    return jax.nn.sigmoid(x)

def _layernorm(x, axis=-1, eps=1e-05):
    m = jnp.mean(x, axis=axis, keepdims=True)
    v = jnp.var(x, axis=axis, keepdims=True)
    return (x - m) / jnp.sqrt(v + eps)

def _scatter_add(tgt, idx, src, axis=0):
    return tgt.at[idx].add(src)

def _segment_sum(src, seg, n):
    return jax.ops.segment_sum(src, seg, n)
kernel_name = 'mk_lm_tower_d2_tok_ids512_r4_ac5a49'

def setup_inputs(seed: int=0):
    np.random.seed(seed)
    _w = jnp.asarray

    def _rec_inputs():
        import jax
        import jax.numpy as jnp
        _rk = jax.random.key(seed)
        x = jax.random.randint(jax.random.fold_in(_rk, 1), (64, 128), 0, 31993, jnp.int32)
        return x
    x = _rec_inputs()

    def _L0_tok_setup():
        import jax, jax.numpy as jnp
        import numpy as np
        V, D, L, F, H, NL = (8000, 128, 1024, 512, 8, 2)
        NB, NHASH, CS = (64, 4, 64)
        DH = D // H
        B, S = (2, 1024)

        def layer_norm(x, scale, bias):
            mu = jnp.mean(x, axis=-1, keepdims=True)
            var = jnp.var(x, axis=-1, keepdims=True)
            return (x - mu) * jax.lax.rsqrt(var + 1e-05) * scale + bias

        def lsh_attention(x, Wqk, Wv, Wo, rots):
            b, s, d = x.shape
            qk = (x @ Wqk).reshape(b, s, H, DH).transpose(0, 2, 1, 3)
            v = (x @ Wv).reshape(b, s, H, DH).transpose(0, 2, 1, 3)
            rot = jnp.einsum('bhsd,hrdk->bhrsk', qk, rots)
            buckets = jnp.argmax(jnp.concatenate([rot, -rot], -1), -1)
            order = jnp.argsort(buckets, axis=-1)
            inv = jnp.argsort(order, axis=-1)
            gather = lambda t: jnp.take_along_axis(jnp.broadcast_to(t[:, :, None], (b, H, NHASH, s, DH)), order[..., None], axis=3)
            sqk = gather(qk).reshape(b, H, NHASH, s // CS, CS, DH)
            sv = gather(v).reshape(b, H, NHASH, s // CS, CS, DH)
            k = sqk / (jnp.linalg.norm(sqk, axis=-1, keepdims=True) + 1e-06)
            kk = jnp.concatenate([k, jnp.roll(k, 1, axis=3)], axis=4)
            vv = jnp.concatenate([sv, jnp.roll(sv, 1, axis=3)], axis=4)
            scores = jnp.einsum('bhrcwd,bhrcud->bhrcwu', sqk, kk) / jnp.sqrt(jnp.float32(DH))
            attn = jax.nn.softmax(scores, axis=-1)
            out = jnp.einsum('bhrcwu,bhrcud->bhrcwd', attn, vv).reshape(b, H, NHASH, s, DH)
            out = jnp.take_along_axis(out, inv[..., None], axis=3).mean(axis=2)
            out = out.transpose(0, 2, 1, 3).reshape(b, s, d)
            return out @ Wo

        def ffn(x, W1, b1, W2, b2):
            return jax.nn.gelu(x @ W1 + b1) @ W2 + b2
        key = jax.random.key(seed)
        ks = jax.random.split(key, 16)
        sd = 0.02
        inp = {'x': jax.random.randint(ks[0], (B, S), 0, V), 'emb': jax.random.normal(ks[1], (V, D), jnp.float32) * sd, 'pos': jax.random.normal(ks[2], (1, L, D), jnp.float32) * sd, 'ln1_s': jnp.ones((NL, D), jnp.float32), 'ln1_b': jnp.zeros((NL, D), jnp.float32), 'Wqk': jax.random.normal(ks[3], (NL, D, D), jnp.float32) * sd, 'Wv': jax.random.normal(ks[4], (NL, D, D), jnp.float32) * sd, 'Wo': jax.random.normal(ks[5], (NL, D, D), jnp.float32) * sd, 'rots': jax.random.normal(ks[6], (NL, H, NHASH, DH, NB // 2), jnp.float32), 'ln2_s': jnp.ones((NL, D), jnp.float32), 'ln2_b': jnp.zeros((NL, D), jnp.float32), 'W1': jax.random.normal(ks[7], (NL, D, F), jnp.float32) * sd, 'b1': jnp.zeros((NL, F), jnp.float32), 'W2': jax.random.normal(ks[8], (NL, F, D), jnp.float32) * sd, 'b2': jnp.zeros((NL, D), jnp.float32)}
        return inp
    _L0_tok_all = _L0_tok_setup()
    _L0_tok_in = {k: v for k, v in _L0_tok_all.items() if k in ('emb', 'pos', 'ln1_s', 'ln1_b', 'Wqk', 'Wv', 'Wo', 'rots', 'ln2_s', 'ln2_b', 'W1', 'b1', 'W2', 'b2')}
    del _L0_tok_all

    def _L0_attn_setup():
        import jax, jax.numpy as jnp
        import numpy as np
        D_MODEL, D_STATE, D_CONV, EXPAND = (128, 16, 2, 2)
        D_INNER = EXPAND * D_MODEL
        DT_RANK = (D_MODEL + 15) // 16
        D_FF = 4 * D_MODEL
        B, L = (8, 512)

        def _mamba_params(key, prefix):
            ks = jax.random.split(key, 6)
            s = lambda k, shape, sc: jax.random.normal(k, shape, jnp.float32) * sc
            return {prefix + 'in_proj': s(ks[0], (2 * D_INNER, D_MODEL), 0.02), prefix + 'conv_w': s(ks[1], (D_INNER, 1, D_CONV), 0.2), prefix + 'conv_b': jnp.zeros((D_INNER,), jnp.float32), prefix + 'x_proj': s(ks[2], (DT_RANK + 2 * D_STATE, D_INNER), 0.02), prefix + 'dt_w': s(ks[3], (D_INNER, DT_RANK), 0.05), prefix + 'dt_b': s(ks[4], (D_INNER,), 0.02) - 4.0, prefix + 'A_log': jnp.log(jnp.broadcast_to(jnp.arange(1, D_STATE + 1, dtype=jnp.float32), (D_INNER, D_STATE))), prefix + 'Dskip': jnp.ones((D_INNER,), jnp.float32), prefix + 'out_proj': s(ks[5], (D_MODEL, D_INNER), 0.02)}

        def _mamba(x, in_proj, conv_w, conv_b, x_proj, dt_w, dt_b, A_log, Dskip, out_proj):
            Bb = x.shape[0]
            xz = jnp.einsum('bld,ed->ble', x, in_proj)
            xi, z = jnp.split(xz, 2, axis=-1)
            xc = jnp.transpose(xi, (0, 2, 1))
            xc = jax.lax.conv_general_dilated(xc, conv_w, (1,), [(D_CONV - 1, 0)], dimension_numbers=('NCH', 'OIH', 'NCH'), feature_group_count=D_INNER)
            xi = jax.nn.silu(jnp.transpose(xc, (0, 2, 1)) + conv_b)
            x_dbl = jnp.einsum('bld,ed->ble', xi, x_proj)
            dt, Bm, Cm = jnp.split(x_dbl, [DT_RANK, DT_RANK + D_STATE], axis=-1)
            dt = jax.nn.softplus(jnp.einsum('blr,dr->bld', dt, dt_w) + dt_b)
            A = -jnp.exp(A_log)

            def step(h, inp):
                u_t, dt_t, B_t, C_t = inp
                dA = jnp.exp(dt_t[..., None] * A)
                h = dA * h + (dt_t * u_t)[..., None] * B_t[:, None, :]
                y = jnp.einsum('bds,bs->bd', h, C_t)
                return (h, y)
            h0 = jnp.zeros((Bb, D_INNER, D_STATE), x.dtype)
            xs = (jnp.swapaxes(xi, 0, 1), jnp.swapaxes(dt, 0, 1), jnp.swapaxes(Bm, 0, 1), jnp.swapaxes(Cm, 0, 1))
            _, ys = jax.lax.scan(step, h0, xs)
            y = jnp.swapaxes(ys, 0, 1) + xi * Dskip
            y = y * jax.nn.silu(z)
            return jnp.einsum('bld,ed->ble', y, out_proj)

        def _ln(x, g, b):
            m = x.mean(-1, keepdims=True)
            v = ((x - m) ** 2).mean(-1, keepdims=True)
            return (x - m) * jax.lax.rsqrt(v + 1e-05) * g + b
        key = jax.random.key(seed)
        kx, kf, kb, k1, k2, k3, k4 = jax.random.split(key, 7)
        inp = {'x': jax.random.normal(kx, (B, L, D_MODEL), jnp.float32)}
        inp.update(_mamba_params(kf, 'f_'))
        inp.update(_mamba_params(kb, 'b_'))
        inp.update({'ffn_w1': jax.random.normal(k1, (D_FF, D_MODEL), jnp.float32) * 0.02, 'ffn_b1': jnp.zeros((D_FF,), jnp.float32), 'ffn_w2': jax.random.normal(k2, (D_MODEL, D_FF), jnp.float32) * 0.02, 'ffn_b2': jnp.zeros((D_MODEL,), jnp.float32), 'ln1_g': jnp.ones((D_MODEL,), jnp.float32), 'ln1_b': jnp.zeros((D_MODEL,), jnp.float32), 'ln2_g': jnp.ones((D_MODEL,), jnp.float32), 'ln2_b': jnp.zeros((D_MODEL,), jnp.float32)})
        return inp
    _L0_attn_all = _L0_attn_setup()
    _L0_attn_in = {k: v for k, v in _L0_attn_all.items() if k in ('f_in_proj', 'f_conv_w', 'f_conv_b', 'f_x_proj', 'f_dt_w', 'f_dt_b', 'f_A_log', 'f_Dskip', 'f_out_proj', 'b_in_proj', 'b_conv_w', 'b_conv_b', 'b_x_proj', 'b_dt_w', 'b_dt_b', 'b_A_log', 'b_Dskip', 'b_out_proj', 'ffn_w1', 'ffn_b1', 'ffn_w2', 'ffn_b2', 'ln1_g', 'ln1_b', 'ln2_g', 'ln2_b')}
    del _L0_attn_all

    def _L0_ffn_setup():
        import jax, jax.numpy as jnp
        import numpy as np
        D_MODEL = 128
        D_FF = 512
        N_EXPERTS = 8
        TOP_K = 2
        key = jax.random.key(seed)
        ks = jax.random.split(key, 7)
        x = jax.random.normal(ks[0], (8, 1024, D_MODEL), dtype=jnp.float32)
        router_w = jax.random.normal(ks[1], (D_MODEL, N_EXPERTS), dtype=jnp.float32) * 0.02
        router_b = jnp.zeros((N_EXPERTS,), dtype=jnp.float32)
        s1 = 1.0 / np.sqrt(D_MODEL)
        s2 = 1.0 / np.sqrt(D_FF)
        w1 = jax.random.uniform(ks[2], (N_EXPERTS, D_MODEL, D_FF), jnp.float32, -s1, s1)
        b1 = jax.random.uniform(ks[3], (N_EXPERTS, D_FF), jnp.float32, -s1, s1)
        w2 = jax.random.uniform(ks[4], (N_EXPERTS, D_FF, D_MODEL), jnp.float32, -s2, s2)
        b2 = jax.random.uniform(ks[5], (N_EXPERTS, D_MODEL), jnp.float32, -s2, s2)
        return {'x': x, 'router_w': router_w, 'router_b': router_b, 'w1': w1, 'b1': b1, 'w2': w2, 'b2': b2}
    _L0_ffn_all = _L0_ffn_setup()
    _L0_ffn_in = {k: v for k, v in _L0_ffn_all.items() if k in ('router_w', 'router_b', 'w1', 'b1', 'w2', 'b2')}
    del _L0_ffn_all

    def _L1_attn_setup():
        import jax, jax.numpy as jnp
        import numpy as np
        D_MODEL = 128
        NUM_HEADS = 8
        D_HEAD = 64
        BATCH = 2
        SEQ = 512
        NEG_BIG = 10000000000.0
        key = jax.random.key(seed)
        k1, k2, k3, k4, k5 = jax.random.split(key, 5)
        scale = D_MODEL ** (-0.5)
        return {'x': jax.random.normal(k1, (BATCH, SEQ, D_MODEL), dtype=jnp.float32), 'W_Q': jax.random.normal(k2, (NUM_HEADS, D_HEAD, D_MODEL), dtype=jnp.float32) * scale, 'W_K': jax.random.normal(k3, (NUM_HEADS, D_HEAD, D_MODEL), dtype=jnp.float32) * scale, 'W_V': jax.random.normal(k4, (NUM_HEADS, D_HEAD, D_MODEL), dtype=jnp.float32) * scale, 'W_O': jax.random.normal(k5, (D_MODEL, D_HEAD * NUM_HEADS), dtype=jnp.float32) * scale}
    _L1_attn_all = _L1_attn_setup()
    _L1_attn_in = {k: v for k, v in _L1_attn_all.items() if k in ('W_Q', 'W_K', 'W_V', 'W_O')}
    del _L1_attn_all

    def _L1_ffn_setup():
        import jax, jax.numpy as jnp
        import numpy as np
        MARK_AX = 0
        OP_AND = 1
        OP_OR = 2
        OP_XOR = 3
        ALU_LO = 16
        ALU_HI = 32
        AX_CARRY_LO = 48
        AX_CARRY_HI = 64
        OUTPUT_LO = 80
        OUTPUT_HI = 96
        NIB_A = 0
        NIB_B = 1
        OP_START = 16
        RESULT = 64
        GE_DIM = 160
        N_ROWS = 8
        B, S, D = (8, 1024, 128)

        def _decode_nibble(x_bd, start):
            bits = x_bd[..., start:start + 16] > 0.5
            return jnp.argmax(bits, axis=-1).astype(x_bd.dtype)

        def _mlp2(x, w1, b1, w2, b2):
            h = jax.nn.relu(jnp.einsum('bsrd,de->bsre', x, w1) + b1)
            return jnp.einsum('bsrd,de->bsre', h, w2) + b2

        def _forward(x_bd, and_w1, and_b1, and_w2, and_b2, or_w1, or_b1, or_w2, or_b2, xor_w1, xor_b1, xor_w2, xor_b2):
            a_lo = _decode_nibble(x_bd, ALU_LO)
            a_hi = _decode_nibble(x_bd, ALU_HI)
            b_lo = _decode_nibble(x_bd, AX_CARRY_LO)
            b_hi = _decode_nibble(x_bd, AX_CARRY_HI)
            Bsz, Ssz, _ = x_bd.shape
            x_ge = jnp.zeros((Bsz, Ssz, N_ROWS, GE_DIM), x_bd.dtype)
            x_ge = x_ge.at[..., 0, NIB_A].set(a_lo).at[..., 1, NIB_A].set(a_hi)
            x_ge = x_ge.at[..., 0, NIB_B].set(b_lo).at[..., 1, NIB_B].set(b_hi)
            x_ge = x_ge.at[..., :, OP_START + 28].set(x_bd[..., OP_OR, None])
            x_ge = x_ge.at[..., :, OP_START + 29].set(x_bd[..., OP_XOR, None])
            x_ge = x_ge.at[..., :, OP_START + 30].set(x_bd[..., OP_AND, None])
            y_and = _mlp2(x_ge, and_w1, and_b1, and_w2, and_b2)
            y_or = _mlp2(x_ge, or_w1, or_b1, or_w2, or_b2)
            y_xor = _mlp2(x_ge, xor_w1, xor_b1, xor_w2, xor_b2)
            is_and = x_bd[..., OP_AND] > 0.5
            is_or = x_bd[..., OP_OR] > 0.5
            is_xor = x_bd[..., OP_XOR] > 0.5
            sel = jnp.where(is_and[..., None, None], y_and, jnp.where(is_or[..., None, None], y_or, y_xor))
            active = (x_bd[..., MARK_AX] >= 0.5) & (is_and | is_or | is_xor)
            res_lo = jnp.clip(jnp.round(sel[..., 0, RESULT]), 0, 15).astype(jnp.int32)
            res_hi = jnp.clip(jnp.round(sel[..., 1, RESULT]), 0, 15).astype(jnp.int32)
            amask = active.astype(x_bd.dtype)[..., None]
            add_lo = 2.0 * jax.nn.one_hot(res_lo, 16, dtype=x_bd.dtype) * amask
            add_hi = 2.0 * jax.nn.one_hot(res_hi, 16, dtype=x_bd.dtype) * amask
            out = x_bd.at[..., OUTPUT_LO:OUTPUT_LO + 16].add(add_lo)
            out = out.at[..., OUTPUT_HI:OUTPUT_HI + 16].add(add_hi)
            return out
        key = jax.random.key(seed)
        ks = jax.random.split(key, 7)
        inp = {'x_bd': jax.random.uniform(ks[0], (B, S, D), dtype=jnp.float32)}
        for i, op in enumerate(['and', 'or', 'xor']):
            inp[op + '_w1'] = jax.random.normal(ks[1 + 2 * i], (GE_DIM, GE_DIM), jnp.float32) * 0.08
            inp[op + '_b1'] = jnp.zeros((GE_DIM,), jnp.float32)
            inp[op + '_w2'] = jax.random.normal(ks[2 + 2 * i], (GE_DIM, GE_DIM), jnp.float32) * 0.08
            inp[op + '_b2'] = jnp.zeros((GE_DIM,), jnp.float32)
        return inp
    _L1_ffn_all = _L1_ffn_setup()
    _L1_ffn_in = {k: v for k, v in _L1_ffn_all.items() if k in ('and_w1', 'and_b1', 'and_w2', 'and_b2', 'or_w1', 'or_b1', 'or_w2', 'or_b2', 'xor_w1', 'xor_b1', 'xor_w2', 'xor_b2')}
    del _L1_ffn_all
    return {'x': x, 'L0_tok_emb': _L0_tok_in['emb'], 'L0_tok_pos': _L0_tok_in['pos'], 'L0_tok_ln1_s': _L0_tok_in['ln1_s'], 'L0_tok_ln1_b': _L0_tok_in['ln1_b'], 'L0_tok_Wqk': _L0_tok_in['Wqk'], 'L0_tok_Wv': _L0_tok_in['Wv'], 'L0_tok_Wo': _L0_tok_in['Wo'], 'L0_tok_rots': _L0_tok_in['rots'], 'L0_tok_ln2_s': _L0_tok_in['ln2_s'], 'L0_tok_ln2_b': _L0_tok_in['ln2_b'], 'L0_tok_W1': _L0_tok_in['W1'], 'L0_tok_b1': _L0_tok_in['b1'], 'L0_tok_W2': _L0_tok_in['W2'], 'L0_tok_b2': _L0_tok_in['b2'], 'L0_attn_f_in_proj': _L0_attn_in['f_in_proj'], 'L0_attn_f_conv_w': _L0_attn_in['f_conv_w'], 'L0_attn_f_conv_b': _L0_attn_in['f_conv_b'], 'L0_attn_f_x_proj': _L0_attn_in['f_x_proj'], 'L0_attn_f_dt_w': _L0_attn_in['f_dt_w'], 'L0_attn_f_dt_b': _L0_attn_in['f_dt_b'], 'L0_attn_f_A_log': _L0_attn_in['f_A_log'], 'L0_attn_f_Dskip': _L0_attn_in['f_Dskip'], 'L0_attn_f_out_proj': _L0_attn_in['f_out_proj'], 'L0_attn_b_in_proj': _L0_attn_in['b_in_proj'], 'L0_attn_b_conv_w': _L0_attn_in['b_conv_w'], 'L0_attn_b_conv_b': _L0_attn_in['b_conv_b'], 'L0_attn_b_x_proj': _L0_attn_in['b_x_proj'], 'L0_attn_b_dt_w': _L0_attn_in['b_dt_w'], 'L0_attn_b_dt_b': _L0_attn_in['b_dt_b'], 'L0_attn_b_A_log': _L0_attn_in['b_A_log'], 'L0_attn_b_Dskip': _L0_attn_in['b_Dskip'], 'L0_attn_b_out_proj': _L0_attn_in['b_out_proj'], 'L0_attn_ffn_w1': _L0_attn_in['ffn_w1'], 'L0_attn_ffn_b1': _L0_attn_in['ffn_b1'], 'L0_attn_ffn_w2': _L0_attn_in['ffn_w2'], 'L0_attn_ffn_b2': _L0_attn_in['ffn_b2'], 'L0_attn_ln1_g': _L0_attn_in['ln1_g'], 'L0_attn_ln1_b': _L0_attn_in['ln1_b'], 'L0_attn_ln2_g': _L0_attn_in['ln2_g'], 'L0_attn_ln2_b': _L0_attn_in['ln2_b'], 'L0_ffn_router_w': _L0_ffn_in['router_w'], 'L0_ffn_router_b': _L0_ffn_in['router_b'], 'L0_ffn_w1': _L0_ffn_in['w1'], 'L0_ffn_b1': _L0_ffn_in['b1'], 'L0_ffn_w2': _L0_ffn_in['w2'], 'L0_ffn_b2': _L0_ffn_in['b2'], 'L1_attn_W_Q': _L1_attn_in['W_Q'], 'L1_attn_W_K': _L1_attn_in['W_K'], 'L1_attn_W_V': _L1_attn_in['W_V'], 'L1_attn_W_O': _L1_attn_in['W_O'], 'L1_ffn_and_w1': _L1_ffn_in['and_w1'], 'L1_ffn_and_b1': _L1_ffn_in['and_b1'], 'L1_ffn_and_w2': _L1_ffn_in['and_w2'], 'L1_ffn_and_b2': _L1_ffn_in['and_b2'], 'L1_ffn_or_w1': _L1_ffn_in['or_w1'], 'L1_ffn_or_b1': _L1_ffn_in['or_b1'], 'L1_ffn_or_w2': _L1_ffn_in['or_w2'], 'L1_ffn_or_b2': _L1_ffn_in['or_b2'], 'L1_ffn_xor_w1': _L1_ffn_in['xor_w1'], 'L1_ffn_xor_b1': _L1_ffn_in['xor_b1'], 'L1_ffn_xor_w2': _L1_ffn_in['xor_w2'], 'L1_ffn_xor_b2': _L1_ffn_in['xor_b2']}

def reference(x, L0_tok_emb, L0_tok_pos, L0_tok_ln1_s, L0_tok_ln1_b, L0_tok_Wqk, L0_tok_Wv, L0_tok_Wo, L0_tok_rots, L0_tok_ln2_s, L0_tok_ln2_b, L0_tok_W1, L0_tok_b1, L0_tok_W2, L0_tok_b2, L0_attn_f_in_proj, L0_attn_f_conv_w, L0_attn_f_conv_b, L0_attn_f_x_proj, L0_attn_f_dt_w, L0_attn_f_dt_b, L0_attn_f_A_log, L0_attn_f_Dskip, L0_attn_f_out_proj, L0_attn_b_in_proj, L0_attn_b_conv_w, L0_attn_b_conv_b, L0_attn_b_x_proj, L0_attn_b_dt_w, L0_attn_b_dt_b, L0_attn_b_A_log, L0_attn_b_Dskip, L0_attn_b_out_proj, L0_attn_ffn_w1, L0_attn_ffn_b1, L0_attn_ffn_w2, L0_attn_ffn_b2, L0_attn_ln1_g, L0_attn_ln1_b, L0_attn_ln2_g, L0_attn_ln2_b, L0_ffn_router_w, L0_ffn_router_b, L0_ffn_w1, L0_ffn_b1, L0_ffn_w2, L0_ffn_b2, L1_attn_W_Q, L1_attn_W_K, L1_attn_W_V, L1_attn_W_O, L1_ffn_and_w1, L1_ffn_and_b1, L1_ffn_and_w2, L1_ffn_and_b2, L1_ffn_or_w1, L1_ffn_or_b1, L1_ffn_or_w2, L1_ffn_or_b2, L1_ffn_xor_w1, L1_ffn_xor_b1, L1_ffn_xor_w2, L1_ffn_xor_b2):
    import jax
    import jax.numpy as jnp

    def _L0_tok_ref(x, emb, pos, ln1_s, ln1_b, Wqk, Wv, Wo, rots, ln2_s, ln2_b, W1, b1, W2, b2):
        import jax, jax.numpy as jnp
        import numpy as np
        V, D, L, F, H, NL = (8000, 128, 1024, 512, 8, 2)
        NB, NHASH, CS = (64, 4, 64)
        DH = D // H
        B, S = (2, 1024)

        def layer_norm(x, scale, bias):
            mu = jnp.mean(x, axis=-1, keepdims=True)
            var = jnp.var(x, axis=-1, keepdims=True)
            return (x - mu) * jax.lax.rsqrt(var + 1e-05) * scale + bias

        def lsh_attention(x, Wqk, Wv, Wo, rots):
            b, s, d = x.shape
            qk = (x @ Wqk).reshape(b, s, H, DH).transpose(0, 2, 1, 3)
            v = (x @ Wv).reshape(b, s, H, DH).transpose(0, 2, 1, 3)
            rot = jnp.einsum('bhsd,hrdk->bhrsk', qk, rots)
            buckets = jnp.argmax(jnp.concatenate([rot, -rot], -1), -1)
            order = jnp.argsort(buckets, axis=-1)
            inv = jnp.argsort(order, axis=-1)
            gather = lambda t: jnp.take_along_axis(jnp.broadcast_to(t[:, :, None], (b, H, NHASH, s, DH)), order[..., None], axis=3)
            sqk = gather(qk).reshape(b, H, NHASH, s // CS, CS, DH)
            sv = gather(v).reshape(b, H, NHASH, s // CS, CS, DH)
            k = sqk / (jnp.linalg.norm(sqk, axis=-1, keepdims=True) + 1e-06)
            kk = jnp.concatenate([k, jnp.roll(k, 1, axis=3)], axis=4)
            vv = jnp.concatenate([sv, jnp.roll(sv, 1, axis=3)], axis=4)
            scores = jnp.einsum('bhrcwd,bhrcud->bhrcwu', sqk, kk) / jnp.sqrt(jnp.float32(DH))
            attn = jax.nn.softmax(scores, axis=-1)
            out = jnp.einsum('bhrcwu,bhrcud->bhrcwd', attn, vv).reshape(b, H, NHASH, s, DH)
            out = jnp.take_along_axis(out, inv[..., None], axis=3).mean(axis=2)
            out = out.transpose(0, 2, 1, 3).reshape(b, s, d)
            return out @ Wo

        def ffn(x, W1, b1, W2, b2):
            return jax.nn.gelu(x @ W1 + b1) @ W2 + b2
        h = emb[x] + pos[:, :x.shape[1], :]
        x1, x2 = (h, jnp.zeros_like(h))
        for l in range(NL):
            y1 = x1 + lsh_attention(layer_norm(x2, ln1_s[l], ln1_b[l]), Wqk[l], Wv[l], Wo[l], rots[l])
            y2 = x2 + ffn(layer_norm(y1, ln2_s[l], ln2_b[l]), W1[l], b1[l], W2[l], b2[l])
            x1, x2 = (y1, y2)
        return (x1 + x2) / 2

    def _L0_attn_ref(x, f_in_proj, f_conv_w, f_conv_b, f_x_proj, f_dt_w, f_dt_b, f_A_log, f_Dskip, f_out_proj, b_in_proj, b_conv_w, b_conv_b, b_x_proj, b_dt_w, b_dt_b, b_A_log, b_Dskip, b_out_proj, ffn_w1, ffn_b1, ffn_w2, ffn_b2, ln1_g, ln1_b, ln2_g, ln2_b):
        import jax, jax.numpy as jnp
        import numpy as np
        D_MODEL, D_STATE, D_CONV, EXPAND = (128, 16, 2, 2)
        D_INNER = EXPAND * D_MODEL
        DT_RANK = (D_MODEL + 15) // 16
        D_FF = 4 * D_MODEL
        B, L = (8, 512)

        def _mamba_params(key, prefix):
            ks = jax.random.split(key, 6)
            s = lambda k, shape, sc: jax.random.normal(k, shape, jnp.float32) * sc
            return {prefix + 'in_proj': s(ks[0], (2 * D_INNER, D_MODEL), 0.02), prefix + 'conv_w': s(ks[1], (D_INNER, 1, D_CONV), 0.2), prefix + 'conv_b': jnp.zeros((D_INNER,), jnp.float32), prefix + 'x_proj': s(ks[2], (DT_RANK + 2 * D_STATE, D_INNER), 0.02), prefix + 'dt_w': s(ks[3], (D_INNER, DT_RANK), 0.05), prefix + 'dt_b': s(ks[4], (D_INNER,), 0.02) - 4.0, prefix + 'A_log': jnp.log(jnp.broadcast_to(jnp.arange(1, D_STATE + 1, dtype=jnp.float32), (D_INNER, D_STATE))), prefix + 'Dskip': jnp.ones((D_INNER,), jnp.float32), prefix + 'out_proj': s(ks[5], (D_MODEL, D_INNER), 0.02)}

        def _mamba(x, in_proj, conv_w, conv_b, x_proj, dt_w, dt_b, A_log, Dskip, out_proj):
            Bb = x.shape[0]
            xz = jnp.einsum('bld,ed->ble', x, in_proj)
            xi, z = jnp.split(xz, 2, axis=-1)
            xc = jnp.transpose(xi, (0, 2, 1))
            xc = jax.lax.conv_general_dilated(xc, conv_w, (1,), [(D_CONV - 1, 0)], dimension_numbers=('NCH', 'OIH', 'NCH'), feature_group_count=D_INNER)
            xi = jax.nn.silu(jnp.transpose(xc, (0, 2, 1)) + conv_b)
            x_dbl = jnp.einsum('bld,ed->ble', xi, x_proj)
            dt, Bm, Cm = jnp.split(x_dbl, [DT_RANK, DT_RANK + D_STATE], axis=-1)
            dt = jax.nn.softplus(jnp.einsum('blr,dr->bld', dt, dt_w) + dt_b)
            A = -jnp.exp(A_log)

            def step(h, inp):
                u_t, dt_t, B_t, C_t = inp
                dA = jnp.exp(dt_t[..., None] * A)
                h = dA * h + (dt_t * u_t)[..., None] * B_t[:, None, :]
                y = jnp.einsum('bds,bs->bd', h, C_t)
                return (h, y)
            h0 = jnp.zeros((Bb, D_INNER, D_STATE), x.dtype)
            xs = (jnp.swapaxes(xi, 0, 1), jnp.swapaxes(dt, 0, 1), jnp.swapaxes(Bm, 0, 1), jnp.swapaxes(Cm, 0, 1))
            _, ys = jax.lax.scan(step, h0, xs)
            y = jnp.swapaxes(ys, 0, 1) + xi * Dskip
            y = y * jax.nn.silu(z)
            return jnp.einsum('bld,ed->ble', y, out_proj)

        def _ln(x, g, b):
            m = x.mean(-1, keepdims=True)
            v = ((x - m) ** 2).mean(-1, keepdims=True)
            return (x - m) * jax.lax.rsqrt(v + 1e-05) * g + b
        x_fwd = _mamba(x, f_in_proj, f_conv_w, f_conv_b, f_x_proj, f_dt_w, f_dt_b, f_A_log, f_Dskip, f_out_proj)
        x_bwd = jnp.flip(_mamba(jnp.flip(x, 1), b_in_proj, b_conv_w, b_conv_b, b_x_proj, b_dt_w, b_dt_b, b_A_log, b_Dskip, b_out_proj), 1)
        x = _ln(x + x_fwd + x_bwd, ln1_g, ln1_b)
        h = jax.nn.gelu(jnp.einsum('bld,fd->blf', x, ffn_w1) + ffn_b1, approximate=False)
        x_ffn = jnp.einsum('blf,df->bld', h, ffn_w2) + ffn_b2
        return _ln(x + x_ffn, ln2_g, ln2_b)

    def _L0_ffn_ref(x, router_w, router_b, w1, b1, w2, b2):
        import jax, jax.numpy as jnp
        import numpy as np
        D_MODEL = 128
        D_FF = 512
        N_EXPERTS = 8
        TOP_K = 2
        leading = x.shape[:-1]
        d = x.shape[-1]
        x_flat = x.reshape(-1, d)
        T = x_flat.shape[0]
        logits = x_flat @ router_w + router_b
        probs = jax.nn.softmax(logits, axis=-1)
        sel_w, sel_idx = jax.lax.top_k(probs, TOP_K)
        sel_w = sel_w / (jnp.sum(sel_w, axis=-1, keepdims=True) + 1e-09)
        tok = jnp.arange(T)
        comb = jnp.zeros((T, N_EXPERTS), dtype=x_flat.dtype)
        for k in range(TOP_K):
            comb = comb.at[tok, sel_idx[:, k]].add(sel_w[:, k])
        out = jnp.zeros_like(x_flat)
        for e in range(N_EXPERTS):
            h = jax.nn.gelu(x_flat @ w1[e] + b1[e], approximate=False)
            y = h @ w2[e] + b2[e]
            out = out + comb[:, e:e + 1] * y
        return out.reshape(*leading, d)

    def _L1_attn_ref(x, W_Q, W_K, W_V, W_O):
        import jax, jax.numpy as jnp
        import numpy as np
        D_MODEL = 128
        NUM_HEADS = 8
        D_HEAD = 64
        BATCH = 2
        SEQ = 512
        NEG_BIG = 10000000000.0
        b, n, d = x.shape
        q = jnp.einsum('ihd,bpd->biph', W_Q, x)
        k = jnp.einsum('ihd,bpd->biph', W_K, x)
        v = jnp.einsum('ihd,bpd->biph', W_V, x)
        scores = jnp.einsum('biph,biqh->biqp', k, q)
        tril = jnp.tril(jnp.ones((n, n), dtype=scores.dtype))
        triu = jnp.triu(jnp.ones((n, n), dtype=scores.dtype))
        masked = scores * tril - NEG_BIG * (1.0 - triu)
        attn = jax.nn.softmax(masked / D_HEAD ** 0.5, axis=-1)
        z = jnp.einsum('biph,biqp->biqh', v, attn)
        z_flat = jnp.transpose(z, (0, 2, 1, 3)).reshape(b, n, -1)
        out = jnp.einsum('df,bqf->bqd', W_O, z_flat)
        return out

    def _L1_ffn_ref(x_bd, and_w1, and_b1, and_w2, and_b2, or_w1, or_b1, or_w2, or_b2, xor_w1, xor_b1, xor_w2, xor_b2):
        import jax, jax.numpy as jnp
        import numpy as np
        MARK_AX = 0
        OP_AND = 1
        OP_OR = 2
        OP_XOR = 3
        ALU_LO = 16
        ALU_HI = 32
        AX_CARRY_LO = 48
        AX_CARRY_HI = 64
        OUTPUT_LO = 80
        OUTPUT_HI = 96
        NIB_A = 0
        NIB_B = 1
        OP_START = 16
        RESULT = 64
        GE_DIM = 160
        N_ROWS = 8
        B, S, D = (8, 1024, 128)

        def _decode_nibble(x_bd, start):
            bits = x_bd[..., start:start + 16] > 0.5
            return jnp.argmax(bits, axis=-1).astype(x_bd.dtype)

        def _mlp2(x, w1, b1, w2, b2):
            h = jax.nn.relu(jnp.einsum('bsrd,de->bsre', x, w1) + b1)
            return jnp.einsum('bsrd,de->bsre', h, w2) + b2

        def _forward(x_bd, and_w1, and_b1, and_w2, and_b2, or_w1, or_b1, or_w2, or_b2, xor_w1, xor_b1, xor_w2, xor_b2):
            a_lo = _decode_nibble(x_bd, ALU_LO)
            a_hi = _decode_nibble(x_bd, ALU_HI)
            b_lo = _decode_nibble(x_bd, AX_CARRY_LO)
            b_hi = _decode_nibble(x_bd, AX_CARRY_HI)
            Bsz, Ssz, _ = x_bd.shape
            x_ge = jnp.zeros((Bsz, Ssz, N_ROWS, GE_DIM), x_bd.dtype)
            x_ge = x_ge.at[..., 0, NIB_A].set(a_lo).at[..., 1, NIB_A].set(a_hi)
            x_ge = x_ge.at[..., 0, NIB_B].set(b_lo).at[..., 1, NIB_B].set(b_hi)
            x_ge = x_ge.at[..., :, OP_START + 28].set(x_bd[..., OP_OR, None])
            x_ge = x_ge.at[..., :, OP_START + 29].set(x_bd[..., OP_XOR, None])
            x_ge = x_ge.at[..., :, OP_START + 30].set(x_bd[..., OP_AND, None])
            y_and = _mlp2(x_ge, and_w1, and_b1, and_w2, and_b2)
            y_or = _mlp2(x_ge, or_w1, or_b1, or_w2, or_b2)
            y_xor = _mlp2(x_ge, xor_w1, xor_b1, xor_w2, xor_b2)
            is_and = x_bd[..., OP_AND] > 0.5
            is_or = x_bd[..., OP_OR] > 0.5
            is_xor = x_bd[..., OP_XOR] > 0.5
            sel = jnp.where(is_and[..., None, None], y_and, jnp.where(is_or[..., None, None], y_or, y_xor))
            active = (x_bd[..., MARK_AX] >= 0.5) & (is_and | is_or | is_xor)
            res_lo = jnp.clip(jnp.round(sel[..., 0, RESULT]), 0, 15).astype(jnp.int32)
            res_hi = jnp.clip(jnp.round(sel[..., 1, RESULT]), 0, 15).astype(jnp.int32)
            amask = active.astype(x_bd.dtype)[..., None]
            add_lo = 2.0 * jax.nn.one_hot(res_lo, 16, dtype=x_bd.dtype) * amask
            add_hi = 2.0 * jax.nn.one_hot(res_hi, 16, dtype=x_bd.dtype) * amask
            out = x_bd.at[..., OUTPUT_LO:OUTPUT_LO + 16].add(add_lo)
            out = out.at[..., OUTPUT_HI:OUTPUT_HI + 16].add(add_hi)
            return out
        return _forward(x_bd, and_w1, and_b1, and_w2, and_b2, or_w1, or_b1, or_w2, or_b2, xor_w1, xor_b1, xor_w2, xor_b2)
    h = _L0_tok_ref(x, L0_tok_emb, L0_tok_pos, L0_tok_ln1_s, L0_tok_ln1_b, L0_tok_Wqk, L0_tok_Wv, L0_tok_Wo, L0_tok_rots, L0_tok_ln2_s, L0_tok_ln2_b, L0_tok_W1, L0_tok_b1, L0_tok_W2, L0_tok_b2)
    h = h + _L0_attn_ref(_layernorm(h, axis=-1), L0_attn_f_in_proj, L0_attn_f_conv_w, L0_attn_f_conv_b, L0_attn_f_x_proj, L0_attn_f_dt_w, L0_attn_f_dt_b, L0_attn_f_A_log, L0_attn_f_Dskip, L0_attn_f_out_proj, L0_attn_b_in_proj, L0_attn_b_conv_w, L0_attn_b_conv_b, L0_attn_b_x_proj, L0_attn_b_dt_w, L0_attn_b_dt_b, L0_attn_b_A_log, L0_attn_b_Dskip, L0_attn_b_out_proj, L0_attn_ffn_w1, L0_attn_ffn_b1, L0_attn_ffn_w2, L0_attn_ffn_b2, L0_attn_ln1_g, L0_attn_ln1_b, L0_attn_ln2_g, L0_attn_ln2_b)
    h = h + _L0_ffn_ref(_layernorm(h, axis=-1), L0_ffn_router_w, L0_ffn_router_b, L0_ffn_w1, L0_ffn_b1, L0_ffn_w2, L0_ffn_b2)
    h = h + _L1_attn_ref(_layernorm(h, axis=-1), L1_attn_W_Q, L1_attn_W_K, L1_attn_W_V, L1_attn_W_O)
    h = h + _L1_ffn_ref(_layernorm(h, axis=-1), L1_ffn_and_w1, L1_ffn_and_b1, L1_ffn_and_w2, L1_ffn_and_b2, L1_ffn_or_w1, L1_ffn_or_b1, L1_ffn_or_w2, L1_ffn_or_b2, L1_ffn_xor_w1, L1_ffn_xor_b1, L1_ffn_xor_w2, L1_ffn_xor_b2)
    return h

_drawn_inputs = setup_inputs


def setup_inputs(seed=0):
    import zlib

    import numpy as np

    out = dict(_drawn_inputs(seed))
    spreads = {'L0_tok_ln1_s': (1.0, 0.2),
     'L0_tok_ln1_b': (0.0, 0.1),
     'L0_tok_ln2_s': (1.0, 0.2),
     'L0_tok_ln2_b': (0.0, 0.1),
     'L0_tok_b1': (0.0, 0.1),
     'L0_tok_b2': (0.0, 0.1),
     'L0_attn_f_conv_b': (0.0, 0.8),
     'L0_attn_f_Dskip': (1.0, 0.6),
     'L0_attn_b_conv_b': (0.0, 0.8),
     'L0_attn_b_Dskip': (1.0, 0.6),
     'L0_attn_ffn_b1': (0.0, 0.317),
     'L0_attn_ffn_b2': (0.0, 0.1),
     'L0_attn_ln1_g': (1.0, 0.2),
     'L0_attn_ln1_b': (0.0, 0.1),
     'L0_attn_ln2_g': (1.0, 0.2),
     'L0_attn_ln2_b': (0.0, 0.1),
     'L0_ffn_router_b': (0.0, 0.1),
     'L1_ffn_and_b1': (0.0, 0.1),
     'L1_ffn_and_b2': (0.0, 0.1),
     'L1_ffn_or_b1': (0.0, 0.777),
     'L1_ffn_or_b2': (0.0, 0.8),
     'L1_ffn_xor_b1': (0.0, 0.1),
     'L1_ffn_xor_b2': (0.0, 0.1)}
    factors = {'L0_tok_Wqk': 39.45,
     'L0_tok_rots': 64.0,
     'L0_attn_f_in_proj': 8.0,
     'L0_attn_f_conv_w': 8.0,
     'L0_attn_f_x_proj': 8.0,
     'L0_attn_f_dt_w': 8.0,
     'L0_attn_f_dt_b': 8.0,
     'L0_attn_f_A_log': 8.0,
     'L0_attn_f_out_proj': 8.0,
     'L0_attn_b_in_proj': 8.0,
     'L0_attn_b_conv_w': 8.0,
     'L0_attn_b_x_proj': 8.0,
     'L0_attn_b_dt_w': 8.0,
     'L0_attn_b_dt_b': 41.424,
     'L0_attn_b_A_log': 8.0,
     'L0_attn_b_out_proj': 8.0,
     'L0_ffn_b1': 5.074,
     'L0_ffn_b2': 3.566,
     'L1_attn_W_Q': 2.934,
     'L1_ffn_or_w1': 8.0,
     'L1_ffn_or_w2': 7.059}
    for name, (base, spread) in spreads.items():
        noise = np.random.default_rng([zlib.crc32(name.encode()), seed]).standard_normal(out[name].shape)
        drawn = base * np.exp(spread * noise) if base else spread * noise
        out[name] = jnp.asarray(drawn.astype(out[name].dtype))
    for name, factor in factors.items():
        out[name] = (out[name] * factor).astype(out[name].dtype)
    return out
```

```python
from contextlib import ExitStack

import numpy as np

import concourse.bass as bass
from concourse import mybir

F32 = mybir.dt.float32
BF16 = mybir.dt.bfloat16
I32 = mybir.dt.int32
ALU = mybir.AluOpType
ACT = mybir.ActivationFunctionType
AX_X = mybir.AxisListType.X

NSEQ, L, D = 64, 128, 128
SEQS = 4
T = SEQS * L
NG = NSEQ // SEQS
V = 8000
TH, TDH = 8, 16
DI, DS, DTR = 256, 16, 8
HALVES = DI // 128
NE = 8
FF = 512
NF = FF // 128
AH, ADH = 8, 64
NIB = ((16, 0, 0), (48, 1, 0), (32, 0, 1), (64, 1, 1))
GE, RESULT = 160, 64
OUT_LO, OUT_HI = 80, 96
TINY = 1e-18
ROUND = 12582912.0
END = 1 << 20
BODY_MAIN = 97
SIDE_BEGIN, SIDE_END = 0, 500

BLOB = (
    [("ident", 128), ("mean", 128), ("headsum", 128), ("pos", L),
     ("wqk0", 128), ("wqk1", 128), ("wv0", 128), ("wv1", 128), ("wo0", 128), ("wo1", 128)]
    + [(f"tw1_{l}", FF) for l in range(2)] + [(f"tw2_{l}", FF) for l in range(2)]
    + [(f"{d}in", 2 * DI) for d in "fb"] + [(f"{d}xbc", HALVES * 96) for d in "fb"]
    + [(f"{d}xdt", HALVES * DTR) for d in "fb"] + [(f"{d}dtw", DI) for d in "fb"]
    + [(f"{d}out", HALVES * 128) for d in "fb"] + [(f"{d}alog", HALVES * DS) for d in "fb"]
    + [("mw1", FF), ("mw2", FF)]
    + [("router", NE), ("routerb", NE), ("before", NE * NE), ("ew1", NE * FF), ("ew2", NE * FF)]
    + [("aq", AH * ADH), ("ak", AH * ADH), ("av", AH * ADH), ("ao", 4 * 128), ("keep", 128), ("push", 128)]
    + [("nibval", 64), ("opsel", 64), ("lw1", 3 * 128 + 96), ("lw2", 6 * 128), ("lw2t", 6 * 128)]
)
COLS = (
    ["eps", "one", "tiny", "small", "mask16", "neg16", "c0"]
    + [f"t{n}{l}" for n in ("l1s", "l1b", "l2s", "l2b", "b2") for l in range(2)]
    + [f"tb1_{l}{c}" for l in range(2) for c in range(NF)]
    + [f"{d}{n}{h}" for d in "fb" for n in ("w0", "w1", "cb", "dtb", "dsk") for h in range(HALVES)]
    + [f"mb1_{c}" for c in range(NF)] + ["mb2", "mg1", "mn1", "mg2", "mn2"]
    + [f"eb1_{e}{c}" for e in range(NE) for c in range(NF)] + [f"eb2_{e}" for e in range(NE)]
    + [f"lb1_{o}" for o in range(4)] + [f"lb2_{o}" for o in range(3)] + ["digit"]
)
AT, n = {}, 0
for name, width in BLOB:
    AT[name] = (n, width)
    n += width
NBLOB = n
COL = {name: i for i, name in enumerate(COLS)}
BITS = [("bcast", 2 * DS * 128), ("fieldcum", 128), ("opcode", 128), ("anyop", 128), ("mark", 128)]
BAT, n = {}, 0
for name, width in BITS:
    BAT[name] = (n, width)
    n += width
NBITS = n


def build(nc, ids_d, emb_d, blob_d, cols_d, bits_d, out_d, groups=NG):
    ctx = ExitStack()

    def sb(name, shape, dt=F32):
        return ctx.enter_context(nc.sbuf_tensor(name, shape, dt))

    W = sb("weights", [128, NBLOB])
    COLT = sb("columns", [128, len(COLS)])
    SEL = sb("selections", [128, NBITS], BF16)
    NEGA = sb("neg_a", [128, 2 * HALVES * DS])

    def w(name, rows=128, a=0, n=None, p0=0):
        at, width = AT[name]
        return W[p0:p0 + rows, at + a:at + a + (width if n is None else n)]

    def col(name, rows=128):
        return COLT[0:rows, COL[name]:COL[name] + 1]

    def sel(name, rows=128, a=0, n=128):
        return SEL[0:rows, BAT[name][0] + a:BAT[name][0] + a + n]

    h_next, h_cur = sb("h_next", [128, T]), sb("h_cur", [128, T])
    h1, h1c = sb("h1", [128, T]), sb("h1c", [128, T])
    m_xin, m_xr, m_x1 = sb("m_xin", [128, T]), sb("m_xr", [128, T]), sb("m_x1", [128, T])
    m_xc, m_sq, m_rs = sb("m_xc", [128, T]), sb("m_sq", [128, T]), sb("m_rs", [128, T])
    m_u = sb("m_u", [128, HALVES, T])
    m_g = sb("m_gate", [128, HALVES, T])
    m_dt = sb("m_dt", [128, HALVES, T])
    m_dtu = sb("m_dtu", [128, HALVES, T])
    m_s = [sb(f"m_s{i}", [128, HALVES, T]) for i in range(3)]
    m_e, m_l, m_d = m_s
    hs = m_s[0]
    dbu = [m_s[1], m_s[2]]
    da = sb("decay", [128, 2, HALVES, T])
    hc = sb("h_times_c", [128, 2, HALVES, T])
    bs = sb("b_rows", [128, 2, T])
    bc3 = sb("bc_parts", [96, T], BF16)
    mid = hc[0:96, 0, 0].bitcast(BF16)[:, 0:T]
    dtr = hc[0:DTR, 0, 1]
    side = sb("side", [128, 25, T])
    s_xc, s_sq, s_rs, s_xn = (side[:, i] for i in range(4))
    idx = sb("id_tile", [128, SEQS], I32)
    idxf = sb("ids_f", [128, 2, SEQS])
    idx2 = sb("row_tile", [128, SEQS], I32)
    small = sb("small", [128, 64])
    bank = [ctx.enter_context(nc.psum_tensor(f"bank{i}", [128, T], F32)) for i in range(8)]
    A, B, C = bank[5], bank[6], bank[7]

    class Semaphores(dict):

        def __missing__(self, name):
            self[name] = ctx.enter_context(nc.semaphore(name))
            return self[name]

    s = Semaphores()
    count = {}

    def tick(ins, name):
        count[name] = count.get(name, 0) + 1
        ins.then_inc(s[name], 1)
        return count[name]

    def link(eng, ins, name):
        eng.wait_ge(s[name], tick(ins, name))

    set_up = ExitStack()
    done = {x: set_up.enter_context(nc.semaphore("set_" + x)) for x in ("cols", "bits", "stage", "w", "a", "v0", "v0s", "c0", "nega", "c0s")}
    with nc.Block() as block:
        @block.sync
        def _(sp):
            sp.dma_start(COLT[:, :], cols_d).then_inc(done["cols"], 16)
            stage = m_s[0][:, :, :].rearrange("p a t -> p (a t)")
            for i in range(0, NBITS, 1024):
                k = min(1024, NBITS - i)
                if i:
                    sp.wait_ge(done["bits"], i // 1024)
                sp.dma_start(stage[:, 0:k], bits_d[:, i:i + k]).then_inc(done["stage"], 16)
            sp.dma_start(W[:, :], blob_d).then_inc(done["w"], 16)

        @block.scalar
        def _(act):
            stage = m_s[0][:, :, :].rearrange("p a t -> p (a t)")
            for i in range(0, NBITS, 1024):
                k = min(1024, NBITS - i)
                act.wait_ge(done["stage"], 16 * (i // 1024 + 1))
                nc.scalar.activation(SEL[:, i:i + k], stage[:, 0:k], ACT.Copy).then_inc(done["bits"], 1)
            act.wait_ge(done["w"], 16)
            n = 2 * HALVES * DS
            nc.scalar.activation(NEGA[:, :], W[:, AT["falog"][0]:AT["falog"][0] + n], ACT.Exp).then_inc(done["a"], 1)

        @block.tensor
        def _(pe):
            pe.wait_ge(done["w"], 16)
            pe.wait_ge(done["cols"], 16)
            nc.tensor.matmul(A[:, 0:1], w("wv0"), col("tl1b0"), start=True, stop=True).then_inc(done["v0"], 1)
            pe.wait_ge(done["v0s"], 1)
            nc.tensor.matmul(A[:, 1:2], w("wo0"), small[:, 0:1], start=True, stop=True).then_inc(done["c0"], 1)

        @block.vector
        def _(dve):
            dve.wait_ge(done["a"], 1)
            nc.vector.tensor_scalar(NEGA[:, :], NEGA[:, :], -1.0, None, ALU.mult).then_inc(done["nega"], 1)
            dve.wait_ge(done["v0"], 1)
            nc.vector.tensor_copy(small[:, 0:1], A[:, 0:1]).then_inc(done["v0s"], 1)
            dve.wait_ge(done["c0"], 1)
            nc.vector.tensor_copy(col("c0"), A[:, 1:2]).then_inc(done["c0s"], 1)

    numbers = sorted(x.num for x in done.values())
    nc.vector.sem_clear(range(numbers[0], numbers[-1] + 1))
    nc.all_engine_barrier()
    set_up.close()

    def body(g_token, do_main, do_tail, g_out, do_token):
        count.clear()

        class Steps:

            def __init__(self, parts):
                self.gen = (t for part in parts for t in part)
                self.at = next(self.gen, END)

            def upto(self, t):
                while self.at <= t:
                    self.at = next(self.gen, END)

        def drive(main, token, tail):
            if do_main:
                m = Steps([main()])
                parts = ([tail()] if do_tail else []) + ([token()] if do_token else [])
                q = Steps(parts)
                first = TAIL0 if do_tail else TOK0
                last = TOK0 + TOKN if do_token else TAIL0 + TAILN
                for k in range(BODY_MAIN):
                    m.upto(k)
                    q.upto(first + (last - first) * (k + 1) // BODY_MAIN)
                m.upto(END - 1)
                q.upto(END - 1)
            else:
                Steps(([tail()] if do_tail else []) + ([token()] if do_token else [])).upto(END - 1)

        TQ = 3 if do_tail else 0
        TAIL0, TAILN, TOK0, TOKN = 100, 230, 400, 70

        block = nc.Block()
        with block:
            @block.tensor
            def _(pe):
                mm = nc.tensor.matmul

                def ln(p, q, t0, x, ready, bk):
                    yield t0
                    pe.wait_ge(s[ready[0]], ready[1])
                    tick(mm(bk[:, :], w("mean"), x, start=True, stop=True), p + "mean")
                    yield t0 + 3
                    pe.wait_ge(s[p + "sq"], q + 1)
                    tick(mm(bk[:, :], w("mean"), s_sq if p != "m_" else m_sq[:, :], start=True, stop=True), p + "var")

                def ffn(p, q, t0, x, w1, w2, gbuf, hb, yb, ready):
                    for c in range(NF + 1):
                        yield t0 + 2 * c
                        if c == 0:
                            pe.wait_ge(s[ready[0]], ready[1])
                        if c < NF:
                            if c >= 2:
                                pe.wait_ge(s[p + "g"], q * NF + c - 1)
                            tick(mm(hb[c % 2][:, :], w(w1, a=128 * c, n=128), x, start=True, stop=True), p + "h")
                        if c:
                            pe.wait_ge(s[p + "g"], q * NF + c)
                            tick(mm(yb[:, :], w(w2, a=128 * (c - 1), n=128), gbuf[:, (c - 1) % 2],
                                    start=(c == 1), stop=(c == NF)), p + "y")

                def token():
                    emb = side[:, 18]
                    y1, y2 = side[:, 4], side[:, 5]
                    gbuf = side[:, 6:8]
                    yield TOK0 + 2
                    for j in range(SEQS):
                        pe.wait_ge(s[f"t_emb{j}"], 16)
                        last = nc.tensor.transpose(A[:, j * L:(j + 1) * L], emb[:, j * D:(j + 1) * D], w("ident"))
                    tick(last, "t_embT")
                    yield from ln("l_", TQ + 0, TOK0 + 4, y1, ("t_y1", 1), A)
                    yield from ffn("t_", 0, TOK0 + 10, s_xn, "tw1_0", "tw2_0", gbuf, (A, B), C, ("l_ln", TQ + 1))
                    yield from ln("l_", TQ + 1, TOK0 + 20, y2, ("t_y2", 1), A)
                    yield TOK0 + 26
                    pe.wait_ge(s["l_ln"], TQ + 2)
                    tick(mm(A[:, :], w("wqk0"), s_xn, start=True, stop=True), "t_q")
                    tick(mm(B[:, :], w("wqk1"), s_xn, start=True, stop=True), "t_q")
                    for j in range(SEQS):
                        last = mm(C[:, j * D:(j + 1) * D], s_xn[:, j * L:(j + 1) * L], w("wv1"), start=True, stop=True)
                    tick(last, "t_v")
                    yield TOK0 + 28
                    for c, bk in enumerate((A, B)):
                        pe.wait_ge(s["t_qsq"], c + 1)
                        tick(mm(bk[:, :], w("headsum"), side[:, 8 + c], start=True, stop=True), "t_n2")
                    qa, ka, E = side[:, 14:16], side[:, 16:18], side[:, 8:10]
                    vaug = side[:, 18:20].rearrange("p a t -> p (a t)")[:, 0:SEQS * TH * 17]\
                        .rearrange("p (j h e) -> p j h e", j=SEQS, h=TH)

                    for it in range(TH + 1):
                        yield TOK0 + 32 + 2 * it
                        if it < TH:
                            c, r = it // 4, slice(32 * (it % 4), 32 * (it % 4) + 32)
                            if it == 0:
                                pe.wait_ge(s["t_ka"], 1)
                            else:
                                pe.wait_ge(s["t_e"], it)
                            for j in range(SEQS):
                                last = mm(A[:, j * L:(j + 1) * L], ka[r, c, j * L:(j + 1) * L],
                                          qa[r, c, j * L:(j + 1) * L], start=True, stop=True)
                            tick(last, "t_s")
                        if it:
                            pe.wait_ge(s["t_e"], it)
                            if it == 1:
                                pe.wait_ge(s["t_va"], 1)
                            for j in range(SEQS):
                                o = C[:, 136 * j + 17 * (it - 1):136 * j + 17 * it] if j < 3 else B[:, 17 * (it - 1):17 * it]
                                last = mm(o, E[:, (it - 1) % 2, j * L:(j + 1) * L], vaug[:, j, it - 1, :],
                                          start=True, stop=True)
                            tick(last, "t_o")
                    yield TOK0 + 51
                    pe.wait_ge(s["t_on"], 1)
                    for j in range(SEQS):
                        last = nc.tensor.transpose(A[:, j * L:(j + 1) * L], side[:, 20, j * D:(j + 1) * D], w("ident"))
                    tick(last, "t_oT")
                    yield TOK0 + 54
                    pe.wait_ge(s["t_oTs"], 1)
                    tick(mm(A[:, :], w("wo1"), side[:, 21], start=True, stop=True), "t_att")
                    yield from ln("l_", TQ + 2, TOK0 + 56, y1, ("t_y1", 2), A)
                    yield from ffn("t_", 1, TOK0 + 62, s_xn, "tw1_1", "tw2_1", gbuf, (A, B), C, ("l_ln", TQ + 3))

                def main():
                    yield from ln("m_", 0, 0, h_cur[:, :], ("m_in", 1), bank[0])
                    for d, dn in enumerate("fb"):
                        t0 = 6 + 34 * d
                        yield t0
                        if d == 0:
                            pe.wait_ge(s["m_ln"], 1)
                        else:
                            pe.wait_ge(s["m_yg"], 1)
                            pe.wait_ge(s["m_hc"], DS)
                            pe.wait_ge(s["m_bs"], DS)
                        for e in range(2 * HALVES):
                            tick(mm(bank[e][:, :], w(dn + "in", a=128 * e, n=128), m_xin[:, :], start=True, stop=True),
                                 "m_xz")
                        yield t0 + 3
                        pe.wait_ge(s["m_u"], 2 * (d + 1))
                        for h in range(HALVES):
                            mm(bank[0][0:96, :], w(dn + "xbc", a=96 * h, n=96), m_u[:, h],
                               start=(h == 0), stop=(h == HALVES - 1))
                        for h in range(HALVES):
                            last = mm(bank[1][0:DTR, :], w(dn + "xdt", a=DTR * h, n=DTR), m_u[:, h],
                                      start=(h == 0), stop=(h == HALVES - 1))
                        tick(last, "m_x")
                        yield t0 + 5
                        pe.wait_ge(s["m_dtr"], d + 1)
                        pe.wait_ge(s["m_gate"], 2 * (d + 1))
                        for h in range(HALVES):
                            tick(mm(bank[2 + h][:, :], w(dn + "dtw", rows=DTR, a=128 * h, n=128), dtr,
                                    start=True, stop=True), "m_dtp")
                        for st in range(DS + 2):
                            yield t0 + 13 + st
                            n = d * DS + st
                            if st == 0:
                                pe.wait_ge(s["m_bc"], d + 1)
                                pe.wait_ge(s["m_v"], d + 1)
                            if st < DS:
                                if st:
                                    pe.wait_ge(s["m_bs"], n)
                                tick(mm(bank[2][:, :], sel("bcast", 96, a=128 * st), bc3[:, :], start=True, stop=True),
                                     "m_b")
                                if st >= 2:
                                    pe.wait_ge(s["m_hc"], n - 1)
                                tick(mm(bank[3 + st % 2][:, :], sel("bcast", 96, a=128 * (DS + st)), bc3[:, :],
                                        start=True, stop=True), "m_c")
                            if st >= 2:
                                pe.wait_ge(s["m_hc"], n - 1)
                                for h in range(HALVES):
                                    last = mm(bank[h][:, :], w("ident"), hc[:, st % 2, h], start=(st == 2),
                                              stop=(st == DS + 1))
                                tick(last, "m_y")
                        yield t0 + 32
                        pe.wait_ge(s["m_yg"], d + 1)
                        for h in range(HALVES):
                            last = mm(bank[4][:, :], w(dn + "out", a=128 * h, n=128), m_g[:, h],
                                      start=(h == 0), stop=(h == HALVES - 1))
                        tick(last, "m_yo")
                    yield from ln("m_", 1, 74, m_xr[:, :], ("m_xr", 2), bank[0])
                    yield from ffn("mf_", 0, 80, m_x1[:, :], "mw1", "mw2", m_u, (bank[0], bank[1]), bank[2], ("m_ln", 2))
                    yield from ln("m_", 2, 90, m_xr[:, :], ("m_xr", 3), bank[0])

                def tail():
                    h2, h3 = side[:, 4], side[:, 5]
                    yield from ln("l_", 0, 100, h1c[:, :], ("e_in", 1), A)
                    yield 106
                    pe.wait_ge(s["l_ln"], 1)
                    for j in range(SEQS):
                        last = mm(A[:, j * NE:(j + 1) * NE], s_xn[:, j * L:(j + 1) * L], w("router"), start=True, stop=True)
                    tick(last, "e_lg")
                    yield 110
                    pe.wait_ge(s["e_comb"], 1)
                    comb = side[:, 11, 0:SEQS * NE]
                    for j in range(SEQS):
                        last = nc.tensor.transpose(B[0:NE, j * L:(j + 1) * L], comb[:, j * NE:(j + 1) * NE], w("ident"))
                    tick(last, "e_cT")
                    gbuf, cT = side[:, 6:8], side[0:NE, 10]
                    for n in range(NE * NF + 1):
                        yield 112 + 2 * n
                        e, c = n // NF, n % NF
                        if n:
                            pe.wait_ge(s["e_g"], n)
                        if n < NE * NF:
                            tick(mm(A[:, :], w("ew1", a=128 * n, n=128), s_xn, start=True, stop=True), "e_h")
                        if n == 0:
                            pe.wait_ge(s["e_cTs"], 1)
                        if n < NE * NF and c == 2:
                            if e:
                                pe.wait_ge(s["e_t"], e)
                            tick(mm(C[:, :], w("ident", rows=NE, a=e, n=1).to_broadcast([NE, 128]), cT, start=True, stop=True), "e_cb")
                        if n:
                            if (n - 1) % NF == 0 and n > 1:
                                pe.wait_ge(s["e_ye"], (n - 1) // NF)
                            tick(mm(B[:, :], w("ew2", a=128 * (n - 1), n=128), gbuf[:, (n - 1) % 2],
                                    start=((n - 1) % NF == 0), stop=((n - 1) % NF == NF - 1)), "e_y")
                    yield from ln("l_", 1, 200, h2, ("e_out", 1), A)
                    q, k, v = side[:, 6:10], side[:, 10:14], side[:, 14:18]
                    for i in range(8):
                        yield 206 + i
                        if i == 0:
                            pe.wait_ge(s["l_ln"], 2)
                        if i >= 2:
                            pe.wait_ge(s["a_ke" if i % 2 else "a_qe"], i // 2)
                        tick(mm((A, B)[i % 2][:, :], w("ak" if i % 2 else "aq", a=128 * (i // 2), n=128), s_xn,
                                start=True, stop=True), "a_qk")
                        if i % 2 == 0:
                            if i:
                                pe.wait_ge(s["a_ve"], i // 2)
                            tick(mm(C[:, :], s_xn[:, i // 2 * L:(i // 2 + 1) * L], w("av"), start=True, stop=True), "a_v")
                    E, ET, zT = side[:, 19], side[:, 20], side[:, 21:25]
                    for i in range(2 * SEQS + 1):
                        yield 216 + 4 * i
                        j, c = i // 2, i % 2
                        if i == 0:
                            pe.wait_ge(s["a_qe"], 4)
                            pe.wait_ge(s["a_ke"], 4)
                        if i < 2 * SEQS:
                            if i:
                                pe.wait_ge(s["a_m"], i)
                            r = slice(64 * c, 64 * c + 64)
                            for pr in range(4):
                                last = mm(A[:, pr * L:(pr + 1) * L], q[r, pr, j * L:(j + 1) * L],
                                          k[r, pr, j * L:(j + 1) * L], start=True, stop=True)
                            tick(last, "a_s")
                        if i:
                            pe.wait_ge(s["a_en"], i)
                            if i >= 2:
                                pe.wait_ge(s["a_et"], i - 1)
                            for h in range(4):
                                last = nc.tensor.transpose(B[:, h * L:(h + 1) * L], E[:, h * L:(h + 1) * L], w("ident"))
                            tick(last, "a_T")
                        yield 218 + 4 * i
                        if i:
                            jj, cc = (i - 1) // 2, (i - 1) % 2
                            pe.wait_ge(s["a_et"], i)
                            if i == 1:
                                pe.wait_ge(s["a_ve"], 4)
                            if cc == 0 and jj:
                                pe.wait_ge(s["a_zc"], jj)
                            for h in range(4):
                                hh = 2 * h + cc
                                last = mm(C[64 * cc:64 * cc + 64, h * L:(h + 1) * L],
                                          v[:, jj, hh * ADH:(hh + 1) * ADH], ET[:, h * L:(h + 1) * L],
                                          start=True, stop=True)
                            tick(last, "a_z")
                    yield 254
                    pe.wait_ge(s["a_zc"], SEQS)
                    for pr in range(4):
                        last = mm(A[:, :], w("ao", a=128 * pr, n=128), zT[:, pr], start=(pr == 0), stop=(pr == 3))
                    tick(last, "a_o")
                    yield from ln("l_", 2, 300, h3, ("a_out", 1), A)
                    bits = side[:, 22].bitcast(BF16)
                    yield 307
                    pe.wait_ge(s["f_b"], 2)
                    tick(mm(A[:, :], sel("fieldcum"), bits[:, 0:T], start=True, stop=True), "f_cnt")
                    tick(mm(B[:, :], sel("opcode"), bits[:, 0:T], start=True, stop=True), "f_cnt")
                    mm(C[:, :], sel("mark"), bits[:, T:2 * T], start=True, stop=False)
                    tick(mm(C[:, :], sel("anyop"), bits[:, 0:T], start=False, stop=True), "f_cnt")
                    yield 309
                    pe.wait_ge(s["f_mask"], 4)
                    mm(A[0:64, :], w("nibval"), side[:, 14], start=True, stop=False)
                    tick(mm(A[0:64, :], w("opsel"), s_xn, start=False, stop=True), "f_xg")
                    xg = side[:, 18]
                    for i in range(8):
                        yield 311 + i
                        r, o = i // 4, i % 4
                        if i == 0:
                            pe.wait_ge(s["f_xgs"], 1)
                        if i >= 2:
                            pe.wait_ge(s["f_rd" if i % 2 else "f_ra"], i // 2)
                        m = 128 if o < 3 else 96
                        tick(mm((B, C)[i % 2][0:m, :], w("lw1", rows=32, a=128 * o, n=m, p0=32 * r),
                                xg[32 * r:32 * r + 32], start=True, stop=True), "f_h")
                    yield 320
                    pe.wait_ge(s["f_ra"], 4)
                    pe.wait_ge(s["f_rd"], 4)
                    for o, bk in enumerate((A, B, C)):
                        for r in range(2):
                            mm(bk[:, :], w("lw2", a=128 * (2 * o + r), n=128), side[:, 6 + 4 * r + o],
                               start=(r == 0), stop=False)
                            last = mm(bk[:, :], w("lw2t", rows=96, a=128 * (2 * o + r), n=128),
                                      side[0:96, 6 + 4 * r + 3], start=False, stop=(r == 1))
                        tick(last, "f_y")
                    yield 323
                    pe.wait_ge(s["f_out"], 1)
                    for j in range(SEQS):
                        last = nc.tensor.transpose(A[:, j * D:(j + 1) * D], side[:, 14, j * L:(j + 1) * L], w("ident"))
                    tick(last, "f_oT")

                drive(main, token, tail)

            @block.scalar
            def _(act):
                af = nc.scalar.activation

                def ln(p, q, t0, bk, xc, sq, rs):
                    yield t0 + 2
                    act.wait_ge(s[p + "xc"], q + 1)
                    tick(af(sq, xc, ACT.Square), p + "sq")
                    yield t0 + 4
                    act.wait_ge(s[p + "var"], q + 1)
                    act.preload_act_table_set("natural_log_exp_and_others")
                    link(act, af(rs, bk[:, :], ACT.Ln, bias=col("eps")), p + "lnv")
                    tick(af(rs, rs, ACT.Exp, scale=-0.5), p + "rstd")

                def ffn(p, q, t0, func, b1, gbuf, hb):
                    for c in range(NF):
                        yield t0 + 2 * c + 1
                        act.wait_ge(s[p + "h"], q * NF + c + 1)
                        if c >= 2:
                            act.wait_ge(s[p + "y"], q * NF + c - 1)
                        tick(af(gbuf[:, c % 2], hb[c % 2][:, :], func, bias=col(b1 + str(c))), p + "g")

                def token():
                    gbuf = side[:, 6:8]
                    lnb = (A, s_xc, s_sq, s_rs)
                    yield from ln("l_", TQ + 0, TOK0 + 4, *lnb)
                    yield from ffn("t_", 0, TOK0 + 10, ACT.Gelu_apprx_tanh, "tb1_0", gbuf, (A, B))
                    yield from ln("l_", TQ + 1, TOK0 + 20, *lnb)
                    yield TOK0 + 27
                    for c, bk in enumerate((A, B)):
                        act.wait_ge(s["t_q"], c + 1)
                        tick(af(side[:, 6 + c], bk[:, :], ACT.Copy), "t_qs")
                        tick(af(side[:, 8 + c], bk[:, :], ACT.Square), "t_qsq")
                    yield TOK0 + 30
                    act.wait_ge(s["t_n2c"], 2)
                    r = side[:, 12:14]
                    link(act, af(r, side[:, 10:12], ACT.Ln), "t_nrm")
                    link(act, af(r, r, ACT.Exp, scale=0.5), "t_nrm")
                    link(act, af(r, r, ACT.Ln, bias=col("small")), "t_nrm")
                    tick(af(r, r, ACT.Exp, scale=-1.0), "t_r")
                    E = side[:, 8:10]
                    for it in range(TH):
                        yield TOK0 + 33 + 2 * it
                        act.wait_ge(s["t_s"], it + 1)
                        if it >= 2:
                            act.wait_ge(s["t_o"], it - 1)
                        if it == 0:
                            act.wait_ge(s["t_ka"], 1)
                        tick(af(E[:, it % 2], A[:, :], ACT.Exp, scale=0.25), "t_e")
                    yield TOK0 + 52
                    act.wait_ge(s["t_oT"], 1)
                    tick(af(side[:, 21], A[:, :], ACT.Copy), "t_oTs")
                    yield from ln("l_", TQ + 2, TOK0 + 56, *lnb)
                    yield from ffn("t_", 1, TOK0 + 62, ACT.Gelu_apprx_tanh, "tb1_1", gbuf, (A, B))

                def main():
                    lnb = (bank[0], m_xc[:, :], m_sq[:, :], m_rs[:, :])
                    yield from ln("m_", 0, 0, *lnb)
                    for d, dn in enumerate("fb"):
                        t0 = 6 + 34 * d
                        yield t0 + 1
                        for h in range(HALVES):
                            act.wait_ge(s["m_xz"], 4 * d + 3 + h)
                            if d:
                                act.wait_ge(s["m_yo"], d)
                            tick(af(m_g[:, h], bank[2 + h][:, :], ACT.Silu), "m_gate")
                        yield t0 + 2
                        for h in range(HALVES):
                            act.wait_ge(s["m_cv"], 2 * d + h + 1)
                            tick(af(m_u[:, h], m_l[:, h], ACT.Silu), "m_u")
                        yield t0 + 4
                        act.wait_ge(s["m_x"], d + 1)
                        if d:
                            act.wait_ge(s["m_c"], DS * d)
                        tick(af(dtr, bank[1][0:DTR, :], ACT.Copy), "m_dtr")
                        tick(af(bc3[:, :], bank[0][0:96, :], ACT.Copy), "m_b1")
                        yield t0 + 6
                        act.wait_ge(s["m_r1"], d + 1)
                        tick(af(mid, m_xc[0:96, :], ACT.Copy), "m_mid")
                        yield t0 + 7
                        act.wait_ge(s["m_v"], d + 1)
                        act.preload_act_table_set("natural_log_exp_and_others")
                        link(act, af(m_e[:, :, :], m_dt[:, :, :], ACT.Abs), "m_sp")
                        link(act, af(m_e[:, :, :], m_e[:, :, :], ACT.Exp, scale=-1.0), "m_ex")
                        tick(af(m_d[:, :, :], m_e[:, :, :], ACT.Identity, scale=-0.5, bias=col("one")), "m_lo")
                        tick(af(m_l[:, :, :], m_e[:, :, :], ACT.Ln, bias=col("one")), "m_l1")
                        lo = 1 - d
                        for st in range(DS):
                            yield t0 + 13 + st
                            n = d * DS + st
                            if st == 0:
                                act.wait_ge(s["m_dtu"], d + 1)
                            act.preload_act_table_set("natural_log_exp_and_others")
                            if st >= 2:
                                act.wait_ge(s["m_scan"], n - 1)
                            for h in range(HALVES):
                                a = (2 * d + h) * DS + st
                                o = da[:, st % 2, h].rearrange("p (j t) -> p j t", j=SEQS)
                                i = m_dt[:, h].rearrange("p (j t) -> p j t", j=SEQS)
                                last = af(o[:, :, lo:lo + L - 1], i[:, :, lo:lo + L - 1], ACT.Exp,
                                          scale=NEGA[:, a:a + 1])
                            tick(last, "m_da")
                            act.wait_ge(s["m_b"], n + 1)
                            if n >= 2:
                                act.wait_ge(s["m_dbu"], n - 1)
                            tick(af(bs[:, st % 2], bank[2][:, :], ACT.Copy), "m_bs")
                    yield from ln("m_", 1, 74, *lnb)
                    yield from ffn("mf_", 0, 80, ACT.Gelu, "mb1_", m_u, (bank[0], bank[1]))
                    yield from ln("m_", 2, 90, *lnb)

                def tail():
                    lnb = (A, s_xc, s_sq, s_rs)
                    yield from ln("l_", 0, 100, *lnb)
                    yield 108
                    act.wait_ge(s["e_lgs"], 1)
                    lg = side[:, 12, 0:SEQS * NE]
                    tick(af(lg, lg, ACT.Exp), "e_ex")
                    yield 111
                    act.wait_ge(s["e_cT"], 1)
                    tick(af(side[0:NE, 10], B[0:NE, :], ACT.Copy), "e_cTs")
                    gbuf = side[:, 6:8]
                    for n in range(NE * NF + 1):
                        yield 113 + 2 * n
                        if n and n % NF == 0:
                            e = n // NF - 1
                            act.wait_ge(s["e_y"], n)
                            if e:
                                act.wait_ge(s["e_t"], e)
                            tick(af(side[:, 8], B[:, :], ACT.Identity, bias=col(f"eb2_{e}")), "e_ye")
                        if n < NE * NF:
                            act.wait_ge(s["e_h"], n + 1)
                            if n >= 2:
                                act.wait_ge(s["e_y"], n - 1)
                            tick(af(gbuf[:, n % 2], A[:, :], ACT.Gelu, bias=col(f"eb1_{n // NF}{n % NF}")), "e_g")
                    yield from ln("l_", 1, 200, *lnb)
                    q, v = side[:, 6:10], side[:, 14:18]
                    for j in range(4):
                        yield 207 + 2 * j
                        act.wait_ge(s["a_qk"], 2 * j + 1)
                        tick(af(q[:, j], A[:, :], ACT.Copy), "a_qe")
                        act.wait_ge(s["a_v"], j + 1)
                        tick(af(v[:, j], C[:, :], ACT.Copy), "a_ve")
                    ms, E, ET = side[:, 18], side[:, 19], side[:, 20]
                    for i in range(2 * SEQS + 1):
                        yield 217 + 4 * i
                        if i:
                            act.wait_ge(s["a_T"], i)
                            if i >= 2:
                                act.wait_ge(s["a_z"], i - 1)
                            tick(af(ET, B[:, :], ACT.Copy), "a_et")
                        yield 218 + 4 * i
                        if i < 2 * SEQS:
                            act.preload_act_table_set("natural_log_exp_and_others")
                            act.wait_ge(s["a_nb"], i + 1)
                            if i:
                                act.wait_ge(s["a_T"], i)
                            for h in range(4):
                                last = af(E[:, h * L:(h + 1) * L], ms[:, h * L:(h + 1) * L], ACT.Exp, scale=0.125,
                                          bias=small[:, 8 + h:9 + h], accum_out=small[:, 16 + h:17 + h])
                            tick(last, "a_e")
                    yield from ln("l_", 2, 300, *lnb)
                    yield 310
                    act.wait_ge(s["f_xg"], 1)
                    tick(af(side[0:64, 18], A[0:64, :], ACT.Copy), "f_xgs")
                    for i in range(0, 8, 2):
                        yield 312 + i
                        o = i % 4
                        act.wait_ge(s["f_h"], i + 1)
                        tick(af(side[:, 6 + i], B[:, :], ACT.Relu, bias=col(f"lb1_{o}")), "f_ra")
                    yield 321
                    for o, bk in enumerate((A, B, C)):
                        act.wait_ge(s["f_y"], o + 1)
                        tick(af(side[:, 19 + o], bk[:, :], ACT.Identity, bias=col(f"lb2_{o}")), "f_ye")
                    yield 324
                    act.wait_ge(s["f_oT"], 1)
                    tick(af(side[:, 23], A[:, :], ACT.Copy), "f_osb")

                drive(main, token, tail)

            @block.vector
            def _(dve):
                tt, ts, stt = nc.vector.tensor_tensor, nc.vector.tensor_scalar, nc.vector.scalar_tensor_tensor

                def ln(p, q, t0, bk, x, xc, rs, out, g=None, b=None):
                    yield t0 + 1
                    dve.wait_ge(s[p + "mean"], q + 1)
                    tick(tt(xc, x, bk[:, :], ALU.subtract), p + "xc")
                    yield t0 + 5
                    dve.wait_ge(s[p + "rstd"], q + 1)
                    if g is None:
                        link(dve, tt(out, xc, rs, ALU.mult), p + "ln")
                    else:
                        link(dve, tt(out, xc, rs, ALU.mult), p + "lnm")
                        link(dve, ts(out, out, col(g), col(b), ALU.mult, ALU.add), p + "ln")

                def token():
                    y1, y2 = side[:, 4], side[:, 5]
                    yield TOK0
                    dve.wait_ge(s["t_ids"], 16)
                    link(dve, ts(idxf[:, 0], idx[:, :], float(-V), float(V - 1), ALU.max, ALU.min), "t_ix")
                    link(dve, ts(idxf[:, 1], idxf[:, 0], 0.0, float(V), ALU.is_lt, ALU.mult), "t_ix")
                    link(dve, tt(idx2[:, :], idxf[:, 0], idxf[:, 1], ALU.add), "t_rows")
                    yield TOK0 + 3
                    dve.wait_ge(s["t_embT"], 1)
                    pos = w("pos").rearrange("p (a t) -> p a t", a=1).to_broadcast([128, SEQS, L])
                    link(dve, stt(y1.rearrange("p (j t) -> p j t", j=SEQS), A[:, :].rearrange("p (j t) -> p j t", j=SEQS),
                                  col("c0"), pos, ALU.add, ALU.add), "t_y1")
                    lnb = (s_xc, s_rs, s_xn)
                    yield from ln("l_", TQ + 0, TOK0 + 4, A, y1, *lnb, "tl2s0", "tl2b0")
                    yield TOK0 + 19
                    dve.wait_ge(s["t_y"], NF)
                    link(dve, ts(y2, C[:, :], col("tb20"), None, ALU.add), "t_y2")
                    yield from ln("l_", TQ + 1, TOK0 + 20, A, y2, *lnb, "tl1s1", "tl1b1")
                    yield TOK0 + 27
                    vaug = side[:, 18:20].rearrange("p a t -> p (a t)")[:, 0:SEQS * TH * 17]\
                        .rearrange("p (j h e) -> p j h e", j=SEQS, h=TH)
                    dve.wait_ge(s["t_v"], 1)
                    nc.vector.memset(vaug[:, :, :, 16:17], 1.0)
                    for j in range(SEQS):
                        last = nc.vector.tensor_copy(vaug[:, j, :, 0:16],
                                                     C[:, j * D:(j + 1) * D].rearrange("p (h e) -> p h e", h=TH))
                    tick(last, "t_va")
                    yield TOK0 + 29
                    for c, bk in enumerate((A, B)):
                        dve.wait_ge(s["t_n2"], c + 1)
                        tick(ts(side[:, 10 + c], bk[:, :], TINY, None, ALU.max), "t_n2c")
                    yield TOK0 + 31
                    dve.wait_ge(s["t_r"], 1)
                    dve.wait_ge(s["t_qs"], 2)
                    q, n2, r, tmp, qa, ka = (side[:, a:a + 2] for a in (6, 10, 12, 8, 14, 16))
                    link(dve, tt(tmp, n2, r, ALU.mult), "t_kq")
                    link(dve, tt(ka, q, r, ALU.mult), "t_kq")
                    link(dve, stt(qa, tmp, col("mask16"), q, ALU.mult, ALU.add), "t_kq")
                    link(dve, ts(ka, ka, col("neg16"), None, ALU.add), "t_ka")
                    yield TOK0 + 50
                    dve.wait_ge(s["t_o"], TH)
                    on = side[:, 20].rearrange("p (j h e) -> p j h e", j=SEQS, h=TH)
                    rc = small[:, 32:64].rearrange("p (j h e) -> p j h e", j=SEQS, e=1)
                    for j in range(SEQS):
                        o = (C[:, 136 * j:136 * j + 136] if j < 3 else B[:, 0:136]).rearrange("p (h e) -> p h e", h=TH)
                        link(dve, nc.vector.reciprocal(rc[:, j], o[:, :, 16:17]), "t_rc")
                        last = tt(on[:, j], o[:, :, 0:16], rc[:, j].to_broadcast([128, TH, 16]), ALU.mult)
                    tick(last, "t_on")
                    yield TOK0 + 55
                    dve.wait_ge(s["t_att"], 1)
                    link(dve, tt(y1, A[:, :], y1, ALU.add), "t_y1")
                    yield from ln("l_", TQ + 2, TOK0 + 56, A, y1, *lnb, "tl2s1", "tl2b1")
                    yield TOK0 + 71
                    dve.wait_ge(s["t_y"], 2 * NF)
                    link(dve, stt(y2, C[:, :], col("tb21"), y2, ALU.add, ALU.add), "t_y2")
                    link(dve, tt(y2, y1, y2, ALU.add), "t_y2")
                    tick(ts(h_next[:, :], y2, 0.5, None, ALU.mult), "t_out")

                def main():
                    lnb = (m_xc[:, :], m_rs[:, :])
                    yield from ln("m_", 0, 0, bank[0], h_cur[:, :], *lnb, m_xin[:, :])
                    for d, dn in enumerate("fb"):
                        t0 = 6 + 34 * d
                        yield t0 + 1
                        new, old = (slice(1, L), slice(0, L - 1)) if d == 0 else (slice(0, L - 1), slice(1, L))
                        for h in range(HALVES):
                            dve.wait_ge(s["m_xz"], 4 * d + h + 1)
                            link(dve, ts(m_l[:, h], bank[h][:, :], col(f"{dn}w1{h}"), col(f"{dn}cb{h}"),
                                         ALU.mult, ALU.add), "m_c1")
                            o = m_l[:, h].rearrange("p (j t) -> p j t", j=SEQS)
                            i = bank[h][:, :].rearrange("p (j t) -> p j t", j=SEQS)
                            tick(stt(o[:, :, new], i[:, :, old], col(f"{dn}w0{h}"), o[:, :, new], ALU.mult, ALU.add),
                                 "m_cv")
                        yield t0 + 5
                        dve.wait_ge(s["m_b1"], d + 1)
                        link(dve, tt(m_xc[0:96, :], bank[0][0:96, :], bc3[:, :], ALU.subtract), "m_r1")
                        yield t0 + 6
                        for h in range(HALVES):
                            dve.wait_ge(s["m_dtp"], 2 * d + h + 1)
                            last = ts(m_dt[:, h], bank[2 + h][:, :], col(f"{dn}dtb{h}"), None, ALU.add)
                        link(dve, last, "m_v")
                        yield t0 + 7
                        dve.wait_ge(s["m_mid"], d + 1)
                        link(dve, tt(m_xc[0:96, :], m_xc[0:96, :], mid, ALU.subtract), "m_r2")
                        nc.vector.tensor_copy(bc3[64:96, :], m_xc[64:96, :])
                        tick(nc.vector.tensor_copy(bc3[32:64, :], hc[32:64, 0, 0].bitcast(BF16)[:, 0:T]), "m_bc")
                        yield t0 + 12
                        z = 0 if d == 0 else L - 1
                        dz = da[:, :, :, :].rearrange("p b h (j t) -> p (b h j) t", j=SEQS)
                        nc.vector.memset(dz[:, :, z:z + 1], 0.0)
                        dve.wait_ge(s["m_l1"], d + 1)
                        link(dve, tt(m_l[:, :, :], m_l[:, :, :], m_e[:, :, :], ALU.min), "m_k1")
                        dve.wait_ge(s["m_low"], d + 1)
                        link(dve, tt(m_l[:, :, :], m_l[:, :, :], m_d[:, :, :], ALU.max), "m_k1")
                        link(dve, stt(m_dt[:, :, :], m_dt[:, :, :], 0.0, m_l[:, :, :], ALU.max, ALU.add), "m_k1")
                        link(dve, tt(m_dtu[:, :, :], m_dt[:, :, :], m_u[:, :, :], ALU.mult), "m_dtu")
                        step = 1 if d == 0 else -1
                        flat = lambda x: x.rearrange("p h t -> p (h t)")[:, ::step]
                        for st in range(DS):
                            yield t0 + 13 + st
                            n = d * DS + st
                            dve.wait_ge(s["m_da"], n + 1)
                            dve.wait_ge(s["m_dbu"], n + 1)
                            link(dve, nc.vector.tensor_tensor_scan(flat(hs[:, :, :]), flat(da[:, st % 2]),
                                                                   flat(dbu[st % 2][:, :, :]), 0.0, ALU.mult, ALU.add),
                                 "m_scan")
                            dve.wait_ge(s["m_c"], n + 1)
                            if st >= 2:
                                dve.wait_ge(s["m_y"], n - 1)
                            cb = bank[3 + st % 2][:, :].rearrange("p (a t) -> p a t", a=1).to_broadcast([128, HALVES, T])
                            link(dve, tt(hc[:, st % 2], hs[:, :, :], cb, ALU.mult), "m_hc")
                        yield t0 + 31
                        dve.wait_ge(s["m_y"], DS * (d + 1))
                        for h in range(HALVES):
                            last = stt(m_dtu[:, h], m_u[:, h], col(f"{dn}dsk{h}"), bank[h][:, :], ALU.mult, ALU.add)
                        link(dve, last, "m_ys")
                        link(dve, tt(m_g[:, :, :], m_dtu[:, :, :], m_g[:, :, :], ALU.mult), "m_yg")
                        yield t0 + 33
                        dve.wait_ge(s["m_yo"], d + 1)
                        link(dve, tt(m_xr[:, :], bank[4][:, :], (m_xr if d else m_xin)[:, :], ALU.add), "m_xr")
                    yield from ln("m_", 1, 74, bank[0], m_xr[:, :], *lnb, m_x1[:, :], "mg1", "mn1")
                    yield 89
                    dve.wait_ge(s["mf_y"], NF)
                    link(dve, stt(m_xr[:, :], bank[2][:, :], col("mb2"), m_x1[:, :], ALU.add, ALU.add), "m_xr")
                    yield from ln("m_", 2, 90, bank[0], m_xr[:, :], *lnb, m_x1[:, :], "mg2", "mn2")
                    yield 96
                    tick(tt(h1[:, :], m_x1[:, :], h_cur[:, :], ALU.add), "m_out")

                def tail():
                    h2, h3 = side[:, 4], side[:, 5]
                    lnb = (s_xc, s_rs, s_xn)
                    yield from ln("l_", 0, 100, A, h1c[:, :], *lnb)
                    yield 107
                    dve.wait_ge(s["e_lg"], 1)
                    n = SEQS * NE
                    comb = side[:, 11, 0:n].rearrange("p (j e) -> p j e", j=SEQS)
                    lg = side[:, 12, 0:n].rearrange("p (j e) -> p j e", j=SEQS)
                    gt = side[:, 12, 256:512].rearrange("p (j a b) -> p j a b", j=SEQS, a=NE)
                    eq = side[:, 13, 0:256].rearrange("p (j a b) -> p j a b", j=SEQS, a=NE)
                    rank = side[:, 11, 64:64 + n].rearrange("p (j e) -> p j e", j=SEQS)
                    mx = small[:, 24:24 + SEQS].rearrange("p (j a) -> p j a", a=1)
                    mb = mx.to_broadcast([128, SEQS, NE])
                    rb = w("routerb").rearrange("p (a e) -> p a e", a=1).to_broadcast([128, SEQS, NE])
                    pl = A[:, 0:n].rearrange("p (j e) -> p j e", j=SEQS)
                    link(dve, tt(lg, pl, rb, ALU.add), "e_r")
                    link(dve, nc.vector.tensor_reduce(mx, lg, AX_X, ALU.max), "e_r")
                    link(dve, tt(lg, lg, mb, ALU.subtract), "e_lgs")
                    yield 109
                    dve.wait_ge(s["e_ex"], 1)
                    link(dve, nc.vector.tensor_reduce(mx, lg, AX_X, ALU.add), "e_r")
                    link(dve, nc.vector.reciprocal(mx, mx), "e_r")
                    link(dve, tt(lg, lg, mb, ALU.mult), "e_r")
                    pa = lg.rearrange("p j (e a) -> p j e a", a=1).to_broadcast([128, SEQS, NE, NE])
                    pb = lg.rearrange("p j (a e) -> p j a e", a=1).to_broadcast([128, SEQS, NE, NE])
                    tri = w("before").rearrange("p (a x) -> p a x", a=1).to_broadcast([128, SEQS, NE * NE])
                    fl = lambda x: x.rearrange("p j a b -> p j (a b)")
                    tick(tt(gt, pb, pa, ALU.is_gt), "e_r")
                    link(dve, tt(eq, pb, pa, ALU.is_equal), "e_r")
                    link(dve, tt(fl(eq), fl(eq), tri, ALU.mult), "e_r")
                    link(dve, tt(gt, gt, eq, ALU.add), "e_r")
                    link(dve, nc.vector.tensor_reduce(rank.rearrange("p j (e a) -> p j e a", a=1), gt, AX_X, ALU.add), "e_r")
                    link(dve, stt(rank, rank, 2.0, lg, ALU.is_lt, ALU.mult), "e_r")
                    link(dve, nc.vector.tensor_reduce(mx, rank, AX_X, ALU.add), "e_r")
                    link(dve, ts(mx, mx, 1e-9, None, ALU.add), "e_r")
                    link(dve, nc.vector.reciprocal(mx, mx), "e_r")
                    link(dve, tt(comb, rank, mb, ALU.mult), "e_comb")
                    for e in range(NE):
                        yield 114 + 2 * NF * (e + 1)
                        dve.wait_ge(s["e_ye"], e + 1)
                        dve.wait_ge(s["e_cb"], e + 1)
                        link(dve, tt(side[:, 9], side[:, 8], C[:, :], ALU.mult), "e_t")
                        link(dve, tt(h2, h2 if e else h1c[:, :], side[:, 9], ALU.add), "e_out" if e == NE - 1 else "e_acc")
                    yield from ln("l_", 1, 200, A, h2, *lnb)
                    for j in range(4):
                        yield 208 + 2 * j
                        dve.wait_ge(s["a_qk"], 2 * j + 2)
                        tick(nc.vector.tensor_copy(side[:, 10 + j], B[:, :]), "a_ke")
                    ms, E, zT = side[:, 18], side[:, 19], side[:, 21:25]
                    four = lambda x: x.rearrange("p (h t) -> p h t", h=4)
                    keep, push = (w(x).rearrange("p (a t) -> p a t", a=1).to_broadcast([128, 4, L]) for x in ("keep", "push"))
                    mxa, nba, sma = (small[:, a:a + 4].rearrange("p (h a) -> p h a", a=1) for a in (28, 8, 16))
                    for i in range(2 * SEQS + 1):
                        if i < 2 * SEQS:
                            yield 217 + 4 * i
                            dve.wait_ge(s["a_s"], i + 1)
                            if i:
                                dve.wait_ge(s["a_e"], i)
                            link(dve, tt(four(ms), four(A[:, :]), keep, ALU.mult), "a_m")
                            link(dve, tt(four(ms), four(ms), push, ALU.add), "a_ms")
                            link(dve, nc.vector.tensor_reduce(mxa, four(ms), AX_X, ALU.max), "a_ms")
                            link(dve, ts(nba, mxa, -0.125, None, ALU.mult), "a_nb")
                        yield 219 + 4 * i
                        if i and i % 2 == 0:
                            j = i // 2 - 1
                            dve.wait_ge(s["a_z"], i)
                            tick(nc.vector.tensor_copy(zT.rearrange("p a (j t) -> p a j t", j=SEQS)[:, :, j],
                                                       four(C[:, :])), "a_zc")
                        if i < 2 * SEQS:
                            dve.wait_ge(s["a_e"], i + 1)
                            link(dve, nc.vector.reciprocal(mxa, sma), "a_ms")
                            link(dve, tt(four(E), four(E), mxa.to_broadcast([128, 4, L]), ALU.mult), "a_en")
                    yield 255
                    dve.wait_ge(s["a_o"], 1)
                    link(dve, tt(h3, A[:, :], h2, ALU.add), "a_out")
                    yield from ln("l_", 2, 300, A, h3, *lnb)
                    bits = side[:, 22].bitcast(BF16)
                    yield 306
                    tick(ts(bits[:, 0:T], s_xn, 0.5, None, ALU.is_gt), "f_b")
                    link(dve, ts(bits[:, T:2 * T], s_xn, 0.5, None, ALU.is_ge), "f_b")
                    yield 308
                    first, mor, mand, active = side[:, 14], side[:, 15].bitcast(I32), side[:, 16].bitcast(I32), side[:, 17]
                    dve.wait_ge(s["f_cnt"], 3)
                    tick(stt(first, A[:, :], 0.0, bits[:, 0:T], ALU.is_equal, ALU.mult), "f_mask")
                    tick(ts(mor, B[:, :], 1.0, None, ALU.is_equal), "f_mask")
                    tick(ts(mand, B[:, :], 1.5, None, ALU.is_gt), "f_mask")
                    link(dve, ts(active, C[:, :], 4.5, None, ALU.is_gt), "f_mask")
                    for i in range(1, 8, 2):
                        yield 312 + i
                        m = 128 if i % 4 < 3 else 96
                        dve.wait_ge(s["f_h"], i + 1)
                        tick(ts(side[0:m, 6 + i], C[0:m, :], col(f"lb1_{i % 4}", m), 0.0, ALU.add, ALU.max), "f_rd")
                    yield 322
                    dve.wait_ge(s["f_ye"], 3)
                    ya, yo, yx = side[:, 19], side[:, 20], side[:, 21]
                    link(dve, nc.vector.copy_predicated(yx, mor, yo), "f_s")
                    link(dve, nc.vector.copy_predicated(yx, mand, ya), "f_s")
                    link(dve, ts(yx, yx, 0.0, 15.0, ALU.max, ALU.min), "f_s")
                    link(dve, ts(yx, yx, ROUND, -ROUND, ALU.add, ALU.add), "f_s")
                    link(dve, ts(yx, yx, col("digit"), 2.0, ALU.is_equal, ALU.mult), "f_s")
                    link(dve, tt(yx, yx, active, ALU.mult), "f_s")
                    link(dve, tt(first, h3, s_xn, ALU.add), "f_s")
                    link(dve, tt(first, first, yx, ALU.add), "f_out")

                if do_main:
                    tick(nc.vector.tensor_copy(h_cur[:, :], h_next[:, :]), "m_in")
                if do_tail:
                    tick(nc.vector.tensor_copy(h1c[:, :], h1[:, :]), "e_in")
                if do_main:
                    dve.wait_ge(s["m_in"], 1)
                if do_tail:
                    dve.wait_ge(s["e_in"], 1)
                drive(main, token, tail)

            @block.gpsimd
            def _(pool):
                def token():
                    yield TOK0 + 1
                    pool.wait_ge(s["t_rows"], 1)
                    for j in range(SEQS):
                        pool.indirect_dma_start(
                            out=side[:, 18, j * D:(j + 1) * D], out_offset=None, in_=emb_d,
                            in_offset=bass.IndirectOffsetOnAxis(ap=idx2[:, j:j + 1], axis=0)).then_inc(s[f"t_emb{j}"], 16)
                    yield END - 1
                    for j in range(SEQS):
                        pool.wait_ge(s[f"t_emb{j}"], 16)
                    for j in range(SEQS):
                        pool.dma_reset(range(s[f"t_emb{j}"].num, s[f"t_emb{j}"].num + 1))

                def main():
                    for d in range(2):
                        t0 = 6 + 34 * d
                        yield t0 + 9
                        pool.wait_ge(s["m_lo"], d + 1)
                        tick(nc.gpsimd.tensor_tensor(m_d[:, :, :], m_d[:, :, :], m_e[:, :, :], ALU.mult), "m_low")
                        for st in range(DS):
                            yield t0 + 13 + st
                            n = d * DS + st
                            if st == 0:
                                pool.wait_ge(s["m_dtu"], d + 1)
                            pool.wait_ge(s["m_bs"], n + 1)
                            if st >= 2:
                                pool.wait_ge(s["m_scan"], n - 1)
                            b = bs[:, st % 2].rearrange("p (a t) -> p a t", a=1).to_broadcast([128, HALVES, T])
                            tick(nc.gpsimd.tensor_tensor(dbu[st % 2][:, :, :], m_dtu[:, :, :], b, ALU.mult), "m_dbu")

                def tail():
                    return iter(())

                drive(main, token, tail)

            @block.sync
            def _(sp):
                if do_token:
                    sp.dma_start(idx[:, :], ids_d[:, bass.ds(g_token * SEQS, SEQS)]).then_inc(s["t_ids"], 16)
                if do_tail:
                    sp.wait_ge(s["f_osb"], 1)
                    sp.dma_start(out_d[bass.ds(g_out * SEQS, SEQS)].rearrange("j t d -> t j d"),
                                 side[:, 23].rearrange("p (j d) -> p j d", j=SEQS)).then_inc(s["f_done"], 16)
                    sp.wait_ge(s["f_done"], 16)

        numbers = sorted(x.num for x in s.values())
        nc.vector.sem_clear(range(numbers[0], numbers[-1] + 1))
        nc.all_engine_barrier()

    body(0, False, False, 0, True)
    body(1, True, False, 0, True)
    if groups > 2:
        with nc.Fori(1, groups - 1) as g:
            body(g + 1, True, True, g - 1, True)
    body(0, True, True, groups - 2, False)
    body(0, False, True, groups - 1, False)
    ctx.close()


def lay_out(x):
    blob = np.zeros((128, NBLOB), np.float32)
    cols = np.zeros((128, len(COLS)), np.float32)
    bits = np.zeros((128, NBITS), np.float32)

    def put(name, a, p0=0, at=0):
        a = a.reshape(a.shape[0], -1)
        blob[p0:p0 + a.shape[0], AT[name][0] + at:AT[name][0] + at + a.shape[1]] = a

    def chunks(a):
        return a.reshape(-1, 128, a.shape[1]).transpose(1, 0, 2).reshape(128, -1)

    def c(name, a):
        cols[0:np.size(a), COL[name]] = a

    put("ident", np.eye(128))
    put("mean", np.full((128, 128), 1 / 128))
    put("headsum", np.kron(np.eye(4), np.ones((32, 32))))
    put("pos", x["L0_tok_pos"][0, 0:L].T)
    for h in range(TH):
        put(f"wqk{h // 4}", x["L0_tok_Wqk"][1][:, h * TDH:(h + 1) * TDH], at=32 * (h % 4))
    for l in range(2):
        put(f"wv{l}", x["L0_tok_Wv"][l])
        put(f"wo{l}", x["L0_tok_Wo"][l])
        put(f"tw1_{l}", x["L0_tok_W1"][l])
        put(f"tw2_{l}", chunks(x["L0_tok_W2"][l]))
        for n, k in (("l1s", "ln1_s"), ("l1b", "ln1_b"), ("l2s", "ln2_s"), ("l2b", "ln2_b"), ("b2", "b2")):
            c(f"t{n}{l}", x["L0_tok_" + k][l])
        for i in range(NF):
            c(f"tb1_{l}{i}", x["L0_tok_b1"][l][128 * i:128 * i + 128])
    c("eps", np.full(128, 1e-5))
    c("one", np.ones(128))
    c("tiny", np.full(128, TINY))
    c("small", np.full(128, 1e-6))
    row16 = (np.arange(128) % 32 == TDH).astype(np.float32)
    c("mask16", row16)
    c("neg16", np.where(row16 > 0, -1.0, 0.0))
    for d in "fb":
        p = f"L0_attn_{d}_"
        put(d + "in", x[p + "in_proj"].T)
        xp, dtw, al, ow = x[p + "x_proj"].T, x[p + "dt_w"].T, x[p + "A_log"], x[p + "out_proj"].T
        put(d + "dtw", dtw)
        put(d + "out", chunks(ow))
        put(d + "alog", chunks(al))
        for h in range(HALVES):
            r = slice(128 * h, 128 * h + 128)
            put(d + "xdt", xp[r, 0:DTR], at=DTR * h)
            for k in range(3):
                put(d + "xbc", xp[r, DTR:DTR + 2 * DS], at=96 * h + 32 * k)
            c(f"{d}w0{h}", x[p + "conv_w"][r, 0, 0])
            c(f"{d}w1{h}", x[p + "conv_w"][r, 0, 1])
            c(f"{d}cb{h}", x[p + "conv_b"][r])
            c(f"{d}dtb{h}", x[p + "dt_b"][r])
            c(f"{d}dsk{h}", x[p + "Dskip"][r])
    put("mw1", x["L0_attn_ffn_w1"].T)
    put("mw2", chunks(x["L0_attn_ffn_w2"].T))
    for i in range(NF):
        c(f"mb1_{i}", x["L0_attn_ffn_b1"][128 * i:128 * i + 128])
    for n, k in (("mb2", "ffn_b2"), ("mg1", "ln1_g"), ("mn1", "ln1_b"), ("mg2", "ln2_g"), ("mn2", "ln2_b")):
        c(n, x["L0_attn_" + k])
    put("router", x["L0_ffn_router_w"])
    put("routerb", np.broadcast_to(x["L0_ffn_router_b"], (128, NE)))
    put("before", np.broadcast_to(np.tril(np.ones((NE, NE)), -1).reshape(1, -1), (128, NE * NE)))
    for e in range(NE):
        put("ew1", x["L0_ffn_w1"][e], at=FF * e)
        put("ew2", chunks(x["L0_ffn_w2"][e]), at=FF * e)
        c(f"eb2_{e}", x["L0_ffn_b2"][e])
        for i in range(NF):
            c(f"eb1_{e}{i}", x["L0_ffn_b1"][e][128 * i:128 * i + 128])
    put("aq", x["L1_attn_W_Q"].reshape(AH * ADH, D).T)
    put("ak", x["L1_attn_W_K"].reshape(AH * ADH, D).T)
    put("av", x["L1_attn_W_V"].reshape(AH * ADH, D).T)
    put("ao", chunks(x["L1_attn_W_O"].T))
    put("keep", np.tril(np.ones((128, 128))))
    put("push", np.where(np.tril(np.ones((128, 128)), -1) > 0, -1e10, 0.0))
    nib, ops = np.zeros((128, 64)), np.zeros((128, 64))
    cum = np.zeros((128, 128))
    for start, operand, row in NIB:
        nib[start:start + 16, 32 * row + operand] = np.arange(16)
        cum[start:start + 16, start:start + 16] = np.triu(np.ones((16, 16)), 1)
    for row in range(2):
        for i, feature in enumerate((2, 3, 1)):
            ops[feature, 32 * row + 2 + i] = 1.0
    put("nibval", nib)
    put("opsel", ops)
    for o, op in enumerate(("and", "or", "xor")):
        p = f"L1_ffn_{op}_"
        w1, w2, b1, b2 = x[p + "w1"], x[p + "w2"][:, RESULT:RESULT + 1], x[p + "b1"], x[p + "b2"]
        for r in range(2):
            for i, feature in enumerate((0, 1, 44, 45, 46)):
                put("lw1", w1[feature:feature + 1, 0:128], p0=32 * r + i, at=128 * o)
                put("lw1", w1[feature:feature + 1, 128:GE], p0=32 * r + i, at=3 * 128 + 32 * o)
            first = (OUT_LO, OUT_HI)[r]
            put("lw2", np.repeat(w2[0:128], 16, axis=1), at=128 * (2 * o + r) + first)
            put("lw2t", np.repeat(w2[128:GE], 16, axis=1), p0=32 * o, at=128 * (2 * o + r) + first)
        c(f"lb1_{o}", b1[0:128])
        cols[32 * o:32 * o + 32, COL["lb1_3"]] = b1[128:GE]
        c(f"lb2_{o}", np.repeat(b2[RESULT:RESULT + 1], 128))
    digit = np.full(128, -1.0)
    digit[OUT_LO:OUT_LO + 16] = digit[OUT_HI:OUT_HI + 16] = np.arange(16)
    c("digit", digit)

    def bit(name, a, at=0):
        bits[0:a.shape[0], BAT[name][0] + at:BAT[name][0] + at + a.shape[1]] = a

    for i in range(2 * DS):
        m = np.zeros((96, 128))
        m[[i, 32 + i, 64 + i]] = 1.0
        bit("bcast", m, at=128 * i)
    bit("fieldcum", cum)
    m = np.zeros((128, 128))
    m[1], m[2] = 2.0, 1.0
    bit("opcode", m)
    m = np.zeros((128, 128))
    m[1:4] = 1.0
    bit("anyop", m)
    m = np.zeros((128, 128))
    m[0] = 4.0
    bit("mark", m)
    return blob, cols, bits


def kernel(**inputs):
    import concourse.bacc as _bacc
    from concourse.bass_utils import run_bass_kernel_spmd as _run

    x = {k: np.asarray(v) for k, v in inputs.items()}
    blob, cols, bits = lay_out(x)
    arrays = {"ids": np.ascontiguousarray(x["x"].T), "emb": np.ascontiguousarray(x["L0_tok_emb"]),
              "blob": blob, "cols": cols, "bits": bits}
    nc = _bacc.Bacc("TRN2", target_bir_lowering=False, num_devices=1)
    args = [nc.dram_tensor(k, a.shape, mybir.dt.from_np(a.dtype), kind="ExternalInput").ap() for k, a in arrays.items()]
    out = nc.dram_tensor("out", (NSEQ, L, D), F32, kind="ExternalOutput").ap()
    build(nc, *args, out)
    r = _run(nc, [arrays], core_ids=[0])
    return r.results[0]["out"]
```

```python
from contextlib import ExitStack

import numpy as np

import concourse.bass as bass
from concourse import mybir

F32 = mybir.dt.float32
BF16 = mybir.dt.bfloat16
I32 = mybir.dt.int32
ALU = mybir.AluOpType
ACT = mybir.ActivationFunctionType
AX_X = mybir.AxisListType.X

NSEQ, L, D = 64, 128, 128
SEQS = 4
T = SEQS * L
NG = NSEQ // SEQS
V = 8000
TH, TDH = 8, 16
DI, DS, DTR = 256, 16, 8
HALVES = DI // 128
NE = 8
FF = 512
NF = FF // 128
AH, ADH = 8, 64
NIB = ((16, 0, 0), (48, 1, 0), (32, 0, 1), (64, 1, 1))
GE, RESULT = 160, 64
OUT_LO, OUT_HI = 80, 96
TINY = 1e-18
ROUND = 12582912.0
END = 1 << 20
BODY_MAIN = 209
TOK0 = 400
DIR, SCAN = 90, 13
TAIL_STEPS = list(range(100, 157)) + list(range(200, 248)) + list(range(300, 325))
TOKEN_STEPS = list(range(TOK0, TOK0 + 72))
TAIL_DUE = ((0, 0), (8, 7), (22, 21), (58, 38), (93, 55), (99, 63), (121, 73), (133, 89), (167, 104), (188, 117), (209, 130))
TOKEN_DUE = ((0, 0), (22, 10), (71, 20), (100, 26), (133, 39), (164, 52), (187, 62), (209, 72))


def last_steps(steps, due, every, phase):
    out = []
    for k in range(BODY_MAIN):
        u = (k - 6) % DIR - SCAN
        if 6 <= k < 6 + 2 * DIR and 0 <= u < 72:
            k -= (u - phase) % every
        n = int(np.interp(k + 1, [a for a, _ in due], [b for _, b in due]) + 1e-6)
        out.append(steps[n - 1] if n else -1)
    return out


LAST = {"token": last_steps(TOKEN_STEPS, TOKEN_DUE, 4, 0),
        "tail": last_steps(TAIL_STEPS, TAIL_DUE, 4, 2)}

BLOB = (
    [("ident", 128), ("mean", 128), ("headsum", 128), ("pos", L),
     ("wqk0", 128), ("wqk1", 128), ("wv0", 128), ("wv1", 128), ("wo0", 128), ("wo1", 128)]
    + [(f"tw1_{l}", FF) for l in range(2)] + [(f"tw2_{l}", FF) for l in range(2)]
    + [(f"{d}in", 2 * DI) for d in "fb"] + [(f"{d}xbc", HALVES * 96) for d in "fb"]
    + [(f"{d}xdt", HALVES * DTR) for d in "fb"] + [(f"{d}dtw", DI) for d in "fb"]
    + [(f"{d}out", HALVES * 128) for d in "fb"] + [(f"{d}alog", HALVES * DS) for d in "fb"]
    + [("mw1", FF), ("mw2", FF)]
    + [("router", NE), ("routerb", NE), ("before", NE * NE), ("ew1", NE * FF), ("ew2", NE * FF)]
    + [("aq", AH * ADH), ("ak", AH * ADH), ("av", AH * ADH), ("ao", 4 * 128), ("keep", 128), ("push", 128)]
    + [("nibval", 64), ("opsel", 64), ("lw1", 3 * 128 + 96), ("lw2", 6 * 128), ("lw2t", 6 * 128)]
)
COLS = (
    ["eps", "one", "small", "mask16", "neg16", "c0"]
    + [f"t{n}{l}" for n in ("l1s", "l1b", "l2s", "l2b", "b2") for l in range(2)]
    + [f"tb1_{l}{c}" for l in range(2) for c in range(NF)]
    + [f"{d}{n}{h}" for d in "fb" for n in ("w0", "w1", "cb", "dtb", "dsk") for h in range(HALVES)]
    + [f"mb1_{c}" for c in range(NF)] + ["mb2", "mg1", "mn1", "mg2", "mn2"]
    + [f"eb1_{e}{c}" for e in range(NE) for c in range(NF)] + [f"eb2_{e}" for e in range(NE)]
    + [f"lb1_{o}" for o in range(4)] + [f"lb2_{o}" for o in range(3)] + ["digit"]
)
AT, n = {}, 0
for name, width in BLOB:
    AT[name] = (n, width)
    n += width
NBLOB = n
COL = {name: i for i, name in enumerate(COLS)}
BITS = [("bcast", 2 * DS * 128), ("fieldcum", 128), ("opcode", 128), ("anyop", 128), ("mark", 128)]
BAT, n = {}, 0
for name, width in BITS:
    BAT[name] = (n, width)
    n += width
NBITS = n


def build(nc, ids_d, emb_d, blob_d, cols_d, bits_d, out_d, groups=NG):
    ctx = ExitStack()

    def sb(name, shape, dt=F32):
        return ctx.enter_context(nc.sbuf_tensor(name, shape, dt))

    W = sb("weights", [128, NBLOB])
    COLT = sb("columns", [128, len(COLS)])
    SEL = sb("selections", [128, NBITS], BF16)
    NEGA = sb("neg_a", [128, 2 * HALVES * DS])

    def w(name, rows=128, a=0, n=None, p0=0):
        at, width = AT[name]
        return W[p0:p0 + rows, at + a:at + a + (width if n is None else n)]

    def col(name, rows=128):
        return COLT[0:rows, COL[name]:COL[name] + 1]

    def sel(name, rows=128, a=0, n=128):
        return SEL[0:rows, BAT[name][0] + a:BAT[name][0] + a + n]

    h_next, h_cur = sb("h_next", [128, T]), sb("h_cur", [128, T])
    h1 = sb("h1", [128, T])
    m_xin, m_xr = sb("m_xin", [128, T]), sb("m_xr", [128, T])
    m_x1 = m_xin
    y_sum = sb("y_sum", [128, HALVES, T])
    m_xc, m_sq = y_sum[:, 0], y_sum[:, 1]
    m_u = sb("m_u", [128, HALVES, T])
    m_g = sb("m_gate", [128, HALVES, T])
    m_dt = sb("m_dt", [128, HALVES, T])
    m_dtu = sb("m_dtu", [128, HALVES, T])
    m_s = [sb(f"m_s{i}", [128, HALVES, T]) for i in range(3)]
    m_e, m_l, m_d = m_s
    hs = m_s[0]
    dbu = [m_s[1], m_s[2]]
    da = sb("decay", [128, 2, HALVES, T])
    bs = sb("b_rows", [128, 2, T])
    bc3 = sb("bc_parts", [96, T], BF16)
    mid = bs[0:96, 0].bitcast(BF16)[:, 0:T]
    dtr = bs[0:DTR, 1]
    tok = sb("tok", [128, 11, T])
    t_xc, t_sq, t_xn, y1, y2 = (tok[:, i] for i in range(5))
    side = sb("side", [128, 22, T])
    s_xc, s_sq, s_rs, s_xn = (side[:, i] for i in range(4))
    idx = sb("id_tile", [128, SEQS], I32)
    idxf = sb("ids_f", [128, 2, SEQS])
    idx2 = sb("row_tile", [128, SEQS], I32)
    small = sb("small", [128, 64])
    bank = [ctx.enter_context(nc.psum_tensor(f"bank{i}", [128, T], F32)) for i in range(8)]
    P, Q = bank[3], bank[4]
    A, B, C = bank[5], bank[6], bank[7]

    class Semaphores(dict):

        def __missing__(self, name):
            self[name] = ctx.enter_context(nc.semaphore(name))
            return self[name]

    s = Semaphores()
    count = {}

    def tick(ins, name):
        count[name] = count.get(name, 0) + 1
        ins.then_inc(s[name], 1)
        return count[name]

    def link(eng, ins, name):
        eng.wait_ge(s[name], tick(ins, name))

    late = {x: ctx.enter_context(nc.semaphore("late_" + x)) for x in ("bits", "rest", "sel", "a", "nega")}
    set_up = ExitStack()
    done = {x: set_up.enter_context(nc.semaphore("set_" + x)) for x in ("cols", "w", "v0", "v0s", "c0", "c0s")}
    first = AT["fin"][0]
    bits_f = side[:, :, :].rearrange("p a t -> p (a t)")[:, 0:NBITS]
    with nc.Block() as block:
        @block.sync
        def _(sp):
            sp.dma_start(COLT[:, :], cols_d).then_inc(done["cols"], 16)
            sp.dma_start(W[:, 0:first], blob_d[:, 0:first]).then_inc(done["w"], 16)

        @block.tensor
        def _(pe):
            pe.wait_ge(done["w"], 16)
            pe.wait_ge(done["cols"], 16)
            nc.tensor.matmul(A[:, 0:1], w("wv0"), col("tl1b0"), start=True, stop=True).then_inc(done["v0"], 1)
            pe.wait_ge(done["v0s"], 1)
            nc.tensor.matmul(A[:, 1:2], w("wo0"), small[:, 0:1], start=True, stop=True).then_inc(done["c0"], 1)

        @block.vector
        def _(dve):
            dve.wait_ge(done["v0"], 1)
            nc.vector.tensor_copy(small[:, 0:1], A[:, 0:1]).then_inc(done["v0s"], 1)
            dve.wait_ge(done["c0"], 1)
            nc.vector.tensor_copy(col("c0"), A[:, 1:2]).then_inc(done["c0s"], 1)

    numbers = sorted(x.num for x in done.values())
    nc.vector.sem_clear(range(numbers[0], numbers[-1] + 1))
    nc.all_engine_barrier()
    set_up.close()

    def finish():
        with nc.Block() as block:
            @block.scalar
            def _(act):
                act.wait_ge(late["bits"], 16)
                nc.scalar.activation(SEL[:, :], bits_f, ACT.Copy).then_inc(late["sel"], 1)
                act.wait_ge(late["rest"], 16)
                n = 2 * HALVES * DS
                at = AT["falog"][0]
                nc.scalar.activation(NEGA[:, :], W[:, at:at + n], ACT.Exp).then_inc(late["a"], 1)

            @block.vector
            def _(dve):
                dve.wait_ge(late["a"], 1)
                nc.vector.tensor_scalar(NEGA[:, :], NEGA[:, :], -1.0, None, ALU.mult).then_inc(late["nega"], 1)

        numbers = sorted(x.num for x in late.values())
        nc.vector.sem_clear(range(numbers[0], numbers[-1] + 1))
        nc.all_engine_barrier()

    def body(g_token, do_main, do_tail, g_out, do_token):
        count.clear()

        class Steps:

            def __init__(self, parts):
                self.gen = (t for part in parts for t in part)
                self.at = next(self.gen, END)

            def upto(self, t):
                while self.at <= t:
                    at = self.at
                    self.at = next(self.gen, END)
                    assert self.at >= at, "steps out of order"

        def drive(main, token, tail):
            beside = ([(Steps([token()]), TOKEN_STEPS, "token")] if do_token else []) \
                + ([(Steps([tail()]), TAIL_STEPS, "tail")] if do_tail else [])
            if do_main:
                m = Steps([main()])
                for k in range(BODY_MAIN):
                    m.upto(k)
                    for q, steps, kind in beside:
                        q.upto(LAST[kind][k])
                m.upto(END - 1)
            for q, steps, kind in beside:
                q.upto(END - 1)

        block = nc.Block()
        with block:
            @block.tensor
            def _(pe):
                mm = nc.tensor.matmul

                def ln(p, q, t0, x, ready, bk):
                    yield t0
                    if ready:
                        pe.wait_ge(s[ready[0]], ready[1])
                    tick(mm(bk[:, :], w("mean"), x, start=True, stop=True), p + "mean")
                    yield t0 + 3
                    pe.wait_ge(s[p + "sq"], q + 1)
                    tick(mm(bk[:, :], w("mean"), {"l_": s_sq, "m_": m_sq, "n_": t_sq}[p], start=True, stop=True), p + "var")

                def ffn(p, q, t0, x, w1, w2, gbuf, hb, yb, ready):
                    for c in range(NF + 1):
                        yield t0 + 2 * c
                        if c == 0:
                            pe.wait_ge(s[ready[0]], ready[1])
                        if c < NF:
                            lag = 1 if hb[0] is hb[1] else 2
                            if c >= lag:
                                pe.wait_ge(s[p + "g"], q * NF + c + 1 - lag)
                            tick(mm(hb[c % 2][:, :], w(w1, a=128 * c, n=128), x, start=True, stop=True), p + "h")
                        if c:
                            pe.wait_ge(s[p + "g"], q * NF + c)
                            tick(mm(yb[:, :], w(w2, a=128 * (c - 1), n=128), gbuf[:, (c - 1) % 2],
                                    start=(c == 1), stop=(c == NF)), p + "y")

                def token():
                    emb, gbuf = tok[:, 5], tok[:, 5:7]
                    yield TOK0 + 2
                    for j in range(SEQS):
                        pe.wait_ge(s[f"t_emb{j}"], 16)
                        last = nc.tensor.transpose(P[:, j * L:(j + 1) * L], emb[:, j * D:(j + 1) * D], w("ident"))
                    tick(last, "t_embT")
                    yield from ln("n_", 0, TOK0 + 4, y1, ("t_y1", 1), P)
                    yield from ffn("t_", 0, TOK0 + 10, t_xn, "tw1_0", "tw2_0", gbuf, (P, P), Q, ("n_ln", 1))
                    yield from ln("n_", 1, TOK0 + 20, y2, ("t_y2", 1), P)
                    yield TOK0 + 26
                    pe.wait_ge(s["n_ln"], 2)
                    tick(mm(P[:, :], w("wqk0"), t_xn, start=True, stop=True), "t_q")
                    tick(mm(Q[:, :], w("wqk1"), t_xn, start=True, stop=True), "t_q")
                    yield TOK0 + 28
                    pe.wait_ge(s["t_qs"], 1)
                    pe.wait_ge(s["t_qsq"], 1)
                    for j in range(SEQS):
                        last = mm(P[:, j * D:(j + 1) * D], t_xn[:, j * L:(j + 1) * L], w("wv1"), start=True, stop=True)
                    tick(last, "t_v")
                    pe.wait_ge(s["t_qs"], 2)
                    pe.wait_ge(s["t_qsq"], 2)
                    tick(mm(Q[:, :], w("headsum"), tok[:, 7], start=True, stop=True), "t_n2")
                    yield TOK0 + 30
                    pe.wait_ge(s["t_va"], 1)
                    tick(mm(P[:, :], w("headsum"), tok[:, 8], start=True, stop=True), "t_n2")
                    qa, ka, E = tok[:, 5:7], tok[:, 7:9], tok[:, 9:11]
                    vaug = tok[:, 0:2].rearrange("p a t -> p (a t)")[:, 0:SEQS * TH * 17]\
                        .rearrange("p (j h e) -> p j h e", j=SEQS, h=TH)

                    for it in range(TH + 1):
                        yield TOK0 + 32 + 2 * it
                        if it < TH:
                            c, r = it // 4, slice(32 * (it % 4), 32 * (it % 4) + 32)
                            if it == 0:
                                pe.wait_ge(s["t_ka"], 1)
                            else:
                                pe.wait_ge(s["t_e"], it)
                            for j in range(SEQS):
                                last = mm(P[:, j * L:(j + 1) * L], ka[r, c, j * L:(j + 1) * L],
                                          qa[r, c, j * L:(j + 1) * L], start=True, stop=True)
                            tick(last, "t_s")
                        if it:
                            pe.wait_ge(s["t_e"], it)
                            if it == TH // 2 + 1:
                                pe.wait_ge(s["t_on"], 1)
                            for j in range(SEQS):
                                a = 17 * (TH // 2 * j + (it - 1) % (TH // 2))
                                last = mm(Q[:, a:a + 17], E[:, (it - 1) % 2, j * L:(j + 1) * L], vaug[:, j, it - 1, :],
                                          start=True, stop=True)
                            tick(last, "t_o")
                    yield TOK0 + 51
                    pe.wait_ge(s["t_on"], 2)
                    for j in range(SEQS):
                        last = nc.tensor.transpose(P[:, j * L:(j + 1) * L], t_xn[:, j * D:(j + 1) * D], w("ident"))
                    tick(last, "t_oT")
                    yield TOK0 + 54
                    pe.wait_ge(s["t_oTs"], 1)
                    tick(mm(P[:, :], w("wo1"), tok[:, 9], start=True, stop=True), "t_att")
                    yield from ln("n_", 2, TOK0 + 56, y1, ("t_y1", 2), P)
                    yield from ffn("t_", 1, TOK0 + 62, t_xn, "tw1_1", "tw2_1", gbuf, (P, P), Q, ("n_ln", 3))

                def main():
                    yield from ln("m_", 0, 0, h_cur[:, :], ("m_in", 1), bank[0])
                    for d, dn in enumerate("fb"):
                        t0 = 6 + DIR * d
                        yield t0
                        if d == 0:
                            pe.wait_ge(s["m_ln"], 1)
                        else:
                            pe.wait_ge(s["m_xr"], 1)
                            pe.wait_ge(s["m_hc"], DS)
                        for e in range(2 * HALVES):
                            if e == 3:
                                yield t0 + 2
                                pe.wait_ge(s["m_cv"], 2 * d + 1)
                            tick(mm(bank[e % 3][:, :], w(dn + "in", a=128 * e, n=128), m_xin[:, :], start=True, stop=True),
                                 "m_xz")
                        yield t0 + 3
                        pe.wait_ge(s["m_u"], 2 * (d + 1))
                        pe.wait_ge(s["m_gate"], 2 * d + 1)
                        for h in range(HALVES):
                            mm(bank[1][0:96, :], w(dn + "xbc", a=96 * h, n=96), m_u[:, h],
                               start=(h == 0), stop=(h == HALVES - 1))
                        for h in range(HALVES):
                            last = mm(bank[2][0:DTR, :], w(dn + "xdt", a=DTR * h, n=DTR), m_u[:, h],
                                      start=(h == 0), stop=(h == HALVES - 1))
                        tick(last, "m_x")
                        yield t0 + 5
                        pe.wait_ge(s["m_dtr"], d + 1)
                        pe.wait_ge(s["m_gate"], 2 * (d + 1))
                        for h in range(HALVES):
                            tick(mm(bank[2 * h][:, :], w(dn + "dtw", rows=DTR, a=128 * h, n=128), dtr,
                                    start=True, stop=True), "m_dtp")
                        for st in range(DS + 1):
                            n = d * DS + st
                            yield t0 + SCAN + 4 * st
                            if st == 0:
                                pe.wait_ge(s["m_bc"], d + 1)
                                pe.wait_ge(s["m_v"], d + 1)
                            if st < DS:
                                if st:
                                    pe.wait_ge(s["m_bs"], n)
                                tick(mm(bank[0][:, :], sel("bcast", 96, a=128 * st), bc3[:, :], start=True, stop=True),
                                     "m_b")
                            if 1 <= st <= DS:
                                yield t0 + SCAN + 4 * st + 2
                                if st >= 3:
                                    pe.wait_ge(s["m_hc"], n - 2)
                                tick(mm(bank[1 + (st - 1) % 2][:, :], sel("bcast", 96, a=128 * (DS + st - 1)), bc3[:, :],
                                        start=True, stop=True), "m_c")
                        yield t0 + SCAN + 75
                        pe.wait_ge(s["m_yg"], d + 1)
                        for h in range(HALVES):
                            last = mm(bank[0][:, :], w(dn + "out", a=128 * h, n=128), m_g[:, h],
                                      start=(h == 0), stop=(h == HALVES - 1))
                        tick(last, "m_yo")
                    yield from ln("m_", 1, 186, m_xr[:, :], ("m_xr", 2), bank[0])
                    yield from ffn("mf_", 0, 192, m_x1[:, :], "mw1", "mw2", m_u, (bank[0], bank[1]), bank[2], ("m_ln", 2))
                    yield from ln("m_", 2, 202, m_xr[:, :], ("m_xr", 3), bank[0])

                def tail():
                    h2, h3 = side[:, 4], side[:, 5]
                    yield from ln("l_", 0, 100, h1[:, :], None, A)
                    yield 106
                    pe.wait_ge(s["l_ln"], 1)
                    for j in range(SEQS):
                        last = mm(A[:, j * NE:(j + 1) * NE], s_xn[:, j * L:(j + 1) * L], w("router"), start=True, stop=True)
                    tick(last, "e_lg")
                    yield 110
                    pe.wait_ge(s["e_comb"], 1)
                    comb = side[:, 11, 0:SEQS * NE]
                    for j in range(SEQS):
                        last = nc.tensor.transpose(B[0:NE, j * L:(j + 1) * L], comb[:, j * NE:(j + 1) * NE], w("ident"))
                    tick(last, "e_cT")
                    gbuf, cT = side[:, 6:8], side[0:NE, 10]
                    for e in range(NE):
                        yield 112 + e
                        if e == 0:
                            pe.wait_ge(s["e_cTs"], 1)
                        if e >= 2:
                            pe.wait_ge(s["e_cd" if e % 2 else "e_ca"], e // 2)
                        tick(mm((A, C)[e % 2][:, :], w("ident", rows=NE, a=e, n=1).to_broadcast([NE, 128]), cT,
                                start=True, stop=True), "e_cb")
                    for n in range(NE * NF + 2):
                        yield 121 + n
                        if n < NE * NF:
                            if n < 2:
                                pe.wait_ge(s["e_cd" if n % 2 else "e_ca"], 4)
                            else:
                                pe.wait_ge(s["e_g"], n - 1)
                            tick(mm((A, C)[n % 2][:, :], w("ew1", a=128 * n, n=128), s_xn, start=True, stop=True), "e_h")
                        if n >= 2:
                            k = n - 2
                            pe.wait_ge(s["e_g"], k + 1)
                            if k % NF == 0 and k:
                                pe.wait_ge(s["e_t"], k // NF)
                            tick(mm(B[:, :], w("ew2", a=128 * k, n=128), gbuf[:, k % 2],
                                    start=(k % NF == 0), stop=(k % NF == NF - 1)), "e_y")
                    yield from ln("l_", 1, 200, h2, ("e_out", 1), A)
                    q, k, v = side[:, 6:10], side[:, 10:14], side[:, 14:18]
                    for i in range(8):
                        yield 206 + i
                        if i == 0:
                            pe.wait_ge(s["l_ln"], 2)
                        if i >= 2:
                            pe.wait_ge(s["a_ke" if i % 2 else "a_qe"], i // 2)
                        tick(mm((A, B)[i % 2][:, :], w("ak" if i % 2 else "aq", a=128 * (i // 2), n=128), s_xn,
                                start=True, stop=True), "a_qk")
                        if i % 2 == 0:
                            if i:
                                pe.wait_ge(s["a_ve"], i // 2)
                            tick(mm(C[:, :], s_xn[:, i // 2 * L:(i // 2 + 1) * L], w("av"), start=True, stop=True), "a_v")
                    E, ET, zT = (side[:, 0], side[:, 1]), side[:, 5], side[:, 18:22]

                    def scores(i):
                        j, c = i // 2, i % 2
                        if i:
                            pe.wait_ge(s["a_m"], i)
                        r = slice(64 * c, 64 * c + 64)
                        for pr in range(4):
                            last = mm(A[:, pr * L:(pr + 1) * L], q[r, pr, j * L:(j + 1) * L],
                                      k[r, pr, j * L:(j + 1) * L], start=True, stop=True)
                        tick(last, "a_s")

                    for i in range(2 * SEQS + 2):
                        yield 216 + 3 * i
                        if i == 0:
                            pe.wait_ge(s["a_qe"], 4)
                            pe.wait_ge(s["a_ke"], 4)
                            scores(0)
                        if i >= 2:
                            jj, cc = (i - 2) // 2, (i - 2) % 2
                            pe.wait_ge(s["a_et"], i - 1)
                            if i == 2:
                                pe.wait_ge(s["a_ve"], 4)
                            if cc == 0 and jj:
                                pe.wait_ge(s["a_zc"], jj)
                            for h in range(4):
                                hh = 2 * h + cc
                                last = mm(C[64 * cc:64 * cc + 64, h * L:(h + 1) * L],
                                          v[:, jj, hh * ADH:(hh + 1) * ADH], ET[:, h * L:(h + 1) * L],
                                          start=True, stop=True)
                            tick(last, "a_z")
                        yield 217 + 3 * i
                        if i + 1 < 2 * SEQS:
                            scores(i + 1)
                        if 1 <= i <= 2 * SEQS:
                            pe.wait_ge(s["a_en"], i)
                            if i >= 2:
                                pe.wait_ge(s["a_et"], i - 1)
                            for h in range(4):
                                last = nc.tensor.transpose(B[:, h * L:(h + 1) * L],
                                                           E[(i - 1) % 2][:, h * L:(h + 1) * L], w("ident"))
                            tick(last, "a_T")
                    yield 246
                    pe.wait_ge(s["a_zc"], SEQS)
                    for pr in range(4):
                        last = mm(A[:, :], w("ao", a=128 * pr, n=128), zT[:, pr], start=(pr == 0), stop=(pr == 3))
                    tick(last, "a_o")
                    yield from ln("l_", 2, 300, h3, ("a_out", 1), A)
                    bits = side[:, 0].bitcast(BF16)
                    yield 307
                    pe.wait_ge(s["f_b"], 2)
                    tick(mm(A[:, :], sel("fieldcum"), bits[:, 0:T], start=True, stop=True), "f_cnt")
                    tick(mm(B[:, :], sel("opcode"), bits[:, 0:T], start=True, stop=True), "f_cnt")
                    mm(C[:, :], sel("mark"), bits[:, T:2 * T], start=True, stop=False)
                    tick(mm(C[:, :], sel("anyop"), bits[:, 0:T], start=False, stop=True), "f_cnt")
                    yield 309
                    pe.wait_ge(s["f_mask"], 4)
                    mm(A[0:64, :], w("nibval"), side[:, 14], start=True, stop=False)
                    tick(mm(A[0:64, :], w("opsel"), s_xn, start=False, stop=True), "f_xg")
                    xg = side[:, 18]
                    for i in range(8):
                        yield 311 + i
                        r, o = i // 4, i % 4
                        if i == 0:
                            pe.wait_ge(s["f_xgs"], 1)
                        if i >= 2:
                            pe.wait_ge(s["f_rd" if i % 2 else "f_ra"], i // 2)
                        m = 128 if o < 3 else 96
                        tick(mm((B, C)[i % 2][0:m, :], w("lw1", rows=32, a=128 * o, n=m, p0=32 * r),
                                xg[32 * r:32 * r + 32], start=True, stop=True), "f_h")
                    yield 320
                    pe.wait_ge(s["f_ra"], 4)
                    pe.wait_ge(s["f_rd"], 4)
                    for o, bk in enumerate((A, B, C)):
                        for r in range(2):
                            mm(bk[:, :], w("lw2", a=128 * (2 * o + r), n=128), side[:, 6 + 4 * r + o],
                               start=(r == 0), stop=False)
                            last = mm(bk[:, :], w("lw2t", rows=96, a=128 * (2 * o + r), n=128),
                                      side[0:96, 6 + 4 * r + 3], start=False, stop=(r == 1))
                        tick(last, "f_y")
                    yield 323
                    pe.wait_ge(s["f_out"], 1)
                    for j in range(SEQS):
                        last = nc.tensor.transpose(A[:, j * D:(j + 1) * D], side[:, 14, j * L:(j + 1) * L], w("ident"))
                    tick(last, "f_oT")

                drive(main, token, tail)

            @block.scalar
            def _(act):
                held = [None]

                def af(out, in_, func, **more):
                    if func in (ACT.Exp, ACT.Ln):
                        if held[0] != "exp":
                            act.preload_act_table_set("natural_log_exp_and_others")
                        held[0] = "exp"
                    elif func in (ACT.Gelu, ACT.Gelu_apprx_tanh, ACT.Silu):
                        held[0] = func
                    return nc.scalar.activation(out, in_, func, **more)

                def ln(p, q, t0, bk, xc, sq, rs):
                    yield t0 + 2
                    act.wait_ge(s[p + "xc"], q + 1)
                    tick(af(sq, xc, ACT.Square), p + "sq")
                    yield t0 + 4
                    act.wait_ge(s[p + "var"], q + 1)
                    link(act, af(rs, bk[:, :], ACT.Ln, bias=col("eps")), p + "lnv")
                    tick(af(rs, rs, ACT.Exp, scale=-0.5), p + "rstd")

                def ffn(p, q, t0, func, b1, gbuf, hb):
                    for c in range(NF):
                        yield t0 + 2 * c + 1
                        act.wait_ge(s[p + "h"], q * NF + c + 1)
                        if c >= 2:
                            act.wait_ge(s[p + "y"], q * NF + c - 1)
                        tick(af(gbuf[:, c % 2], hb[c % 2][:, :], func, bias=col(b1 + str(c))), p + "g")

                def token():
                    gbuf = tok[:, 5:7]
                    lnb = (P, t_xc, t_sq, t_sq)
                    yield from ln("n_", 0, TOK0 + 4, *lnb)
                    yield from ffn("t_", 0, TOK0 + 10, ACT.Gelu_apprx_tanh, "tb1_0", gbuf, (P, P))
                    yield from ln("n_", 1, TOK0 + 20, *lnb)
                    yield TOK0 + 27
                    for c, bk in enumerate((P, Q)):
                        act.wait_ge(s["t_q"], c + 1)
                        tick(af(tok[:, 5 + c], bk[:, :], ACT.Copy), "t_qs")
                        tick(af(tok[:, 7 + c], bk[:, :], ACT.Square), "t_qsq")
                    yield TOK0 + 30
                    act.wait_ge(s["t_n2c"], 2)
                    r = tok[:, 7:9]
                    link(act, af(r, tok[:, 9:11], ACT.Ln), "t_nrm")
                    link(act, af(r, r, ACT.Exp, scale=0.5), "t_nrm")
                    link(act, af(r, r, ACT.Ln, bias=col("small")), "t_nrm")
                    tick(af(r, r, ACT.Exp, scale=-1.0), "t_r")
                    E = tok[:, 9:11]
                    for it in range(TH):
                        yield TOK0 + 33 + 2 * it
                        act.wait_ge(s["t_s"], it + 1)
                        if it >= 2:
                            act.wait_ge(s["t_o"], it - 1)
                        if it == 0:
                            act.wait_ge(s["t_ka"], 1)
                        tick(af(E[:, it % 2], P[:, :], ACT.Exp, scale=0.25), "t_e")
                    yield TOK0 + 52
                    act.wait_ge(s["t_oT"], 1)
                    tick(af(tok[:, 9], P[:, :], ACT.Copy), "t_oTs")
                    yield from ln("n_", 2, TOK0 + 56, *lnb)
                    yield from ffn("t_", 1, TOK0 + 62, ACT.Gelu_apprx_tanh, "tb1_1", gbuf, (P, P))

                def main():
                    lnb = (bank[0], m_xc, m_sq, m_sq)
                    yield from ln("m_", 0, 0, *lnb)
                    for d, dn in enumerate("fb"):
                        t0 = 6 + DIR * d

                        def gate(h):
                            act.wait_ge(s["m_xz"], 4 * d + 3 + h)
                            if d:
                                act.wait_ge(s["m_yo"], d)
                            tick(af(m_g[:, h], bank[2 - 2 * h][:, :], ACT.Silu), "m_gate")

                        yield t0 + 1
                        gate(0)
                        yield t0 + 2
                        for h in range(HALVES):
                            act.wait_ge(s["m_cv"], 2 * d + h + 1)
                            tick(af(m_u[:, h], m_l[:, h], ACT.Silu), "m_u")
                        gate(1)
                        yield t0 + 4
                        act.wait_ge(s["m_x"], d + 1)
                        if d:
                            act.wait_ge(s["m_c"], DS * d)
                            act.wait_ge(s["m_dbu"], DS * d)
                        tick(af(dtr, bank[2][0:DTR, :], ACT.Copy), "m_dtr")
                        tick(af(bc3[:, :], bank[1][0:96, :], ACT.Copy), "m_b1")
                        yield t0 + 6
                        act.wait_ge(s["m_r1"], d + 1)
                        tick(af(mid, m_xc[0:96, :], ACT.Copy), "m_mid")
                        yield t0 + 7
                        act.wait_ge(s["m_v"], d + 1)
                        link(act, af(m_e[:, :, :], m_dt[:, :, :], ACT.Abs), "m_sp")
                        link(act, af(m_e[:, :, :], m_e[:, :, :], ACT.Exp, scale=-1.0), "m_ex")
                        tick(af(m_d[:, :, :], m_e[:, :, :], ACT.Identity, scale=-0.5, bias=col("one")), "m_lo")
                        tick(af(m_l[:, :, :], m_e[:, :, :], ACT.Ln, bias=col("one")), "m_l1")
                        lo = 1 - d
                        for st in range(DS):
                            n = d * DS + st
                            yield t0 + SCAN + 4 * st + 2
                            act.wait_ge(s["m_b"], n + 1)
                            if n >= 2:
                                act.wait_ge(s["m_dbu"], n - 1)
                            tick(af(bs[:, st % 2], bank[0][:, :], ACT.Copy), "m_bs")
                            if st == 0:
                                act.wait_ge(s["m_dtu"], d + 1)
                            for h in range(HALVES):
                                yield t0 + SCAN + 4 * st + 3 + h
                                if h == 0 and st >= 2:
                                    act.wait_ge(s["m_scan"], n - 1)
                                a = (2 * d + h) * DS + st
                                o = da[:, st % 2, h].rearrange("p (j t) -> p j t", j=SEQS)
                                i = m_dt[:, h].rearrange("p (j t) -> p j t", j=SEQS)
                                last = af(o[:, :, lo:lo + L - 1], i[:, :, lo:lo + L - 1], ACT.Exp,
                                          scale=NEGA[:, a:a + 1])
                            tick(last, "m_da")
                    yield from ln("m_", 1, 186, *lnb)
                    yield from ffn("mf_", 0, 192, ACT.Gelu, "mb1_", m_u, (bank[0], bank[1]))
                    yield from ln("m_", 2, 202, *lnb)

                def tail():
                    lnb = (A, s_xc, s_sq, s_rs)
                    yield from ln("l_", 0, 100, *lnb)
                    yield 108
                    act.wait_ge(s["e_lgs"], 1)
                    lg = side[:, 12, 0:SEQS * NE]
                    tick(af(lg, lg, ACT.Exp), "e_ex")
                    yield 111
                    act.wait_ge(s["e_cT"], 1)
                    tick(af(side[0:NE, 10], B[0:NE, :], ACT.Copy), "e_cTs")
                    gbuf = side[:, 6:8]
                    for e in range(0, NE, 2):
                        yield 113 + e
                        act.wait_ge(s["e_cb"], e + 1)
                        tick(af(side[:, 14 + e], A[:, :], ACT.Copy), "e_ca")
                    for n in range(NE * NF):
                        yield 122 + n
                        act.wait_ge(s["e_h"], n + 1)
                        if n >= 2:
                            act.wait_ge(s["e_y"], n - 1)
                        tick(af(gbuf[:, n % 2], (A, C)[n % 2][:, :], ACT.Gelu, bias=col(f"eb1_{n // NF}{n % NF}")), "e_g")
                    yield from ln("l_", 1, 200, *lnb)
                    q, v = side[:, 6:10], side[:, 14:18]
                    for j in range(4):
                        yield 207 + 2 * j
                        act.wait_ge(s["a_qk"], 2 * j + 1)
                        tick(af(q[:, j], A[:, :], ACT.Copy), "a_qe")
                        act.wait_ge(s["a_v"], j + 1)
                        tick(af(v[:, j], C[:, :], ACT.Copy), "a_ve")
                    ms, E, ET = (side[:, 2], side[:, 3]), (side[:, 0], side[:, 1]), side[:, 5]
                    for i in range(2 * SEQS + 1):
                        yield 218 + 3 * i
                        if i < 2 * SEQS:
                            act.wait_ge(s["a_nb"], i + 1)
                            if i >= 2:
                                act.wait_ge(s["a_T"], i - 1)
                            for h in range(4):
                                k = 4 * (i % 2) + h
                                last = af(E[i % 2][:, h * L:(h + 1) * L], ms[i % 2][:, h * L:(h + 1) * L], ACT.Exp,
                                          scale=0.125, bias=small[:, 8 + k:9 + k], accum_out=small[:, 16 + k:17 + k])
                            tick(last, "a_e")
                        if i:
                            act.wait_ge(s["a_T"], i)
                            if i >= 2:
                                act.wait_ge(s["a_z"], i - 1)
                            tick(af(ET, B[:, :], ACT.Copy), "a_et")
                    yield from ln("l_", 2, 300, *lnb)
                    yield 310
                    act.wait_ge(s["f_xg"], 1)
                    tick(af(side[0:64, 18], A[0:64, :], ACT.Copy), "f_xgs")
                    for i in range(0, 8, 2):
                        yield 312 + i
                        o = i % 4
                        act.wait_ge(s["f_h"], i + 1)
                        tick(af(side[:, 6 + i], B[:, :], ACT.Relu, bias=col(f"lb1_{o}")), "f_ra")
                    yield 321
                    for o, bk in enumerate((A, B, C)):
                        act.wait_ge(s["f_y"], o + 1)
                        tick(af(side[:, 19 + o], bk[:, :], ACT.Identity, bias=col(f"lb2_{o}")), "f_ye")
                    yield 324
                    act.wait_ge(s["f_oT"], 1)
                    tick(af(side[:, 1], A[:, :], ACT.Copy), "f_osb")

                drive(main, token, tail)

            @block.vector
            def _(dve):
                tt, ts, stt = nc.vector.tensor_tensor, nc.vector.tensor_scalar, nc.vector.scalar_tensor_tensor

                def ln(p, q, t0, bk, x, xc, rs, out, g=None, b=None):
                    yield t0 + 1
                    dve.wait_ge(s[p + "mean"], q + 1)
                    tick(tt(xc, x, bk[:, :], ALU.subtract), p + "xc")
                    yield t0 + 5
                    dve.wait_ge(s[p + "rstd"], q + 1)
                    if g is None:
                        link(dve, tt(out, xc, rs, ALU.mult), p + "ln")
                    else:
                        link(dve, tt(out, xc, rs, ALU.mult), p + "lnm")
                        link(dve, ts(out, out, col(g), col(b), ALU.mult, ALU.add), p + "ln")

                def token():
                    yield TOK0
                    dve.wait_ge(s["t_ids"], 16)
                    link(dve, ts(idxf[:, 0], idx[:, :], float(-V), float(V - 1), ALU.max, ALU.min), "t_ix")
                    link(dve, ts(idxf[:, 1], idxf[:, 0], 0.0, float(V), ALU.is_lt, ALU.mult), "t_ix")
                    link(dve, tt(idx2[:, :], idxf[:, 0], idxf[:, 1], ALU.add), "t_rows")
                    yield TOK0 + 3
                    dve.wait_ge(s["t_embT"], 1)
                    pos = w("pos").rearrange("p (a t) -> p a t", a=1).to_broadcast([128, SEQS, L])
                    link(dve, stt(y1.rearrange("p (j t) -> p j t", j=SEQS), P[:, :].rearrange("p (j t) -> p j t", j=SEQS),
                                  col("c0"), pos, ALU.add, ALU.add), "t_y1")
                    lnb = (t_xc, t_sq, t_xn)
                    yield from ln("n_", 0, TOK0 + 4, P, y1, *lnb, "tl2s0", "tl2b0")
                    yield TOK0 + 19
                    dve.wait_ge(s["t_y"], NF)
                    link(dve, ts(y2, Q[:, :], col("tb20"), None, ALU.add), "t_y2")
                    yield from ln("n_", 1, TOK0 + 20, P, y2, *lnb, "tl1s1", "tl1b1")
                    yield TOK0 + 29
                    vaug = tok[:, 0:2].rearrange("p a t -> p (a t)")[:, 0:SEQS * TH * 17]\
                        .rearrange("p (j h e) -> p j h e", j=SEQS, h=TH)
                    dve.wait_ge(s["t_v"], 1)
                    nc.vector.memset(vaug[:, :, :, 16:17], 1.0)
                    for j in range(SEQS):
                        last = nc.vector.tensor_copy(vaug[:, j, :, 0:16],
                                                     P[:, j * D:(j + 1) * D].rearrange("p (h e) -> p h e", h=TH))
                    tick(last, "t_va")
                    for c, bk in enumerate((Q, P)):
                        if c:
                            yield TOK0 + 30
                        dve.wait_ge(s["t_n2"], c + 1)
                        tick(ts(tok[:, 9 + c], bk[:, :], TINY, None, ALU.max), "t_n2c")
                    yield TOK0 + 31
                    dve.wait_ge(s["t_r"], 1)
                    q, r, n2 = tok[:, 5:7], tok[:, 7:9], tok[:, 9:11]
                    link(dve, tt(n2, n2, r, ALU.mult), "t_kq")
                    link(dve, tt(r, q, r, ALU.mult), "t_kq")
                    link(dve, stt(q, n2, col("mask16"), q, ALU.mult, ALU.add), "t_kq")
                    link(dve, ts(r, r, col("neg16"), None, ALU.add), "t_ka")
                    on = t_xn.rearrange("p (j h e) -> p j h e", j=SEQS, h=TH)
                    rc = small[:, 40:56].rearrange("p (j h e) -> p j h e", j=SEQS, e=1)
                    o = Q[:, 0:17 * 4 * SEQS].rearrange("p (j h e) -> p j h e", j=SEQS, e=17)
                    for half in range(2):
                        yield (TOK0 + 41, TOK0 + 50)[half]
                        dve.wait_ge(s["t_o"], 4 * (half + 1))
                        link(dve, nc.vector.reciprocal(rc, o[:, :, :, 16:17]), "t_rc")
                        for j in range(SEQS):
                            last = tt(on[:, j, 4 * half:4 * half + 4], o[:, j, :, 0:16],
                                      rc[:, j].to_broadcast([128, 4, 16]), ALU.mult)
                        link(dve, last, "t_on")
                    yield TOK0 + 55
                    dve.wait_ge(s["t_att"], 1)
                    link(dve, tt(y1, P[:, :], y1, ALU.add), "t_y1")
                    yield from ln("n_", 2, TOK0 + 56, P, y1, *lnb, "tl2s1", "tl2b1")
                    yield TOK0 + 71
                    dve.wait_ge(s["t_y"], 2 * NF)
                    link(dve, stt(y2, Q[:, :], col("tb21"), y2, ALU.add, ALU.add), "t_y2")
                    link(dve, tt(y2, y1, y2, ALU.add), "t_y2")
                    tick(ts(h_next[:, :], y2, 0.5, None, ALU.mult), "t_out")

                def main():
                    lnb = (m_xc, m_sq)
                    yield from ln("m_", 0, 0, bank[0], h_cur[:, :], *lnb, m_xin[:, :])
                    for d, dn in enumerate("fb"):
                        t0 = 6 + DIR * d
                        yield t0 + 1
                        new, old = (slice(1, L), slice(0, L - 1)) if d == 0 else (slice(0, L - 1), slice(1, L))
                        for h in range(HALVES):
                            dve.wait_ge(s["m_xz"], 4 * d + h + 1)
                            link(dve, ts(m_l[:, h], bank[h][:, :], col(f"{dn}w1{h}"), col(f"{dn}cb{h}"),
                                         ALU.mult, ALU.add), "m_c1")
                            o = m_l[:, h].rearrange("p (j t) -> p j t", j=SEQS)
                            i = bank[h][:, :].rearrange("p (j t) -> p j t", j=SEQS)
                            tick(stt(o[:, :, new], i[:, :, old], col(f"{dn}w0{h}"), o[:, :, new], ALU.mult, ALU.add),
                                 "m_cv")
                        yield t0 + 5
                        dve.wait_ge(s["m_b1"], d + 1)
                        link(dve, tt(m_xc[0:96, :], bank[1][0:96, :], bc3[:, :], ALU.subtract), "m_r1")
                        yield t0 + 6
                        for h in range(HALVES):
                            dve.wait_ge(s["m_dtp"], 2 * d + h + 1)
                            last = ts(m_dt[:, h], bank[2 * h][:, :], col(f"{dn}dtb{h}"), None, ALU.add)
                        link(dve, last, "m_v")
                        yield t0 + 7
                        dve.wait_ge(s["m_mid"], d + 1)
                        link(dve, tt(m_xc[0:96, :], m_xc[0:96, :], mid, ALU.subtract), "m_r2")
                        nc.vector.tensor_copy(bc3[64:96, :], m_xc[64:96, :])
                        tick(nc.vector.tensor_copy(bc3[32:64, :], bs[32:64, 0].bitcast(BF16)[:, 0:T]), "m_bc")
                        yield t0 + 12
                        z = 0 if d == 0 else L - 1
                        dz = da[:, :, :, :].rearrange("p b h (j t) -> p (b h j) t", j=SEQS)
                        nc.vector.memset(dz[:, :, z:z + 1], 0.0)
                        dve.wait_ge(s["m_l1"], d + 1)
                        link(dve, tt(m_l[:, :, :], m_l[:, :, :], m_e[:, :, :], ALU.min), "m_k1")
                        dve.wait_ge(s["m_low"], d + 1)
                        link(dve, tt(m_l[:, :, :], m_l[:, :, :], m_d[:, :, :], ALU.max), "m_k1")
                        link(dve, stt(m_dt[:, :, :], m_dt[:, :, :], 0.0, m_l[:, :, :], ALU.max, ALU.add), "m_k1")
                        link(dve, tt(m_dtu[:, :, :], m_dt[:, :, :], m_u[:, :, :], ALU.mult), "m_dtu")
                        step = 1 if d == 0 else -1
                        flat = lambda x: x.rearrange("p h t -> p (h t)")[:, ::step]

                        def add(st):
                            dve.wait_ge(s["m_hc"], d * DS + st + 1)
                            if st > 1:
                                dve.wait_ge(s["m_y"], d * (DS - 1) + st - 1)
                            link(dve, tt(y_sum[:, :, :], y_sum[:, :, :], hs[:, :, :], ALU.add), "m_y")

                        for st in range(DS):
                            yield t0 + SCAN + 4 * st + 8
                            n = d * DS + st
                            if st > 1:
                                add(st - 1)
                            dve.wait_ge(s["m_da"], n + 1)
                            dve.wait_ge(s["m_dbu"], n + 1)
                            if n:
                                dve.wait_ge(s["m_hc"], n)
                            tick(nc.vector.tensor_tensor_scan(flat(hs[:, :, :]), flat(da[:, st % 2]),
                                                              flat(dbu[st % 2][:, :, :]), 0.0, ALU.mult, ALU.add),
                                 "m_scan")
                            yield t0 + SCAN + 4 * st + 10
                            dve.wait_ge(s["m_scan"], n + 1)
                            dve.wait_ge(s["m_c"], n + 1)
                            cb = bank[1 + st % 2][:, :].rearrange("p (a t) -> p a t", a=1).to_broadcast([128, HALVES, T])
                            tick(tt(hs[:, :, :] if st else y_sum[:, :, :], hs[:, :, :], cb, ALU.mult), "m_hc")
                        yield t0 + SCAN + 74
                        add(DS - 1)
                        for h in range(HALVES):
                            last = stt(m_dtu[:, h], m_u[:, h], col(f"{dn}dsk{h}"), y_sum[:, h], ALU.mult, ALU.add)
                        link(dve, last, "m_ys")
                        link(dve, tt(m_g[:, :, :], m_dtu[:, :, :], m_g[:, :, :], ALU.mult), "m_yg")
                        yield t0 + SCAN + 76
                        dve.wait_ge(s["m_yo"], d + 1)
                        link(dve, tt(m_xr[:, :], bank[0][:, :], (m_xr if d else m_xin)[:, :], ALU.add), "m_xr")
                    yield from ln("m_", 1, 186, bank[0], m_xr[:, :], *lnb, m_x1[:, :], "mg1", "mn1")
                    yield 201
                    dve.wait_ge(s["mf_y"], NF)
                    link(dve, stt(m_xr[:, :], bank[2][:, :], col("mb2"), m_x1[:, :], ALU.add, ALU.add), "m_xr")
                    yield from ln("m_", 2, 202, bank[0], m_xr[:, :], *lnb, m_x1[:, :], "mg2", "mn2")
                    yield 208
                    if do_tail:
                        dve.wait_ge(s["e_acc"], 1)
                    tick(tt(h1[:, :], m_x1[:, :], h_cur[:, :], ALU.add), "m_out")

                def tail():
                    h2, h3 = side[:, 4], side[:, 5]
                    lnb = (s_xc, s_rs, s_xn)
                    yield from ln("l_", 0, 100, A, h1[:, :], *lnb)
                    yield 107
                    dve.wait_ge(s["e_lg"], 1)
                    n = SEQS * NE
                    comb = side[:, 11, 0:n].rearrange("p (j e) -> p j e", j=SEQS)
                    lg = side[:, 12, 0:n].rearrange("p (j e) -> p j e", j=SEQS)
                    gt = side[:, 12, 256:512].rearrange("p (j a b) -> p j a b", j=SEQS, a=NE)
                    eq = side[:, 13, 0:256].rearrange("p (j a b) -> p j a b", j=SEQS, a=NE)
                    rank = side[:, 11, 64:64 + n].rearrange("p (j e) -> p j e", j=SEQS)
                    mx = small[:, 36:36 + SEQS].rearrange("p (j a) -> p j a", a=1)
                    mb = mx.to_broadcast([128, SEQS, NE])
                    rb = w("routerb").rearrange("p (a e) -> p a e", a=1).to_broadcast([128, SEQS, NE])
                    pl = A[:, 0:n].rearrange("p (j e) -> p j e", j=SEQS)
                    link(dve, tt(lg, pl, rb, ALU.add), "e_r")
                    link(dve, nc.vector.tensor_reduce(mx, lg, AX_X, ALU.max), "e_r")
                    link(dve, tt(lg, lg, mb, ALU.subtract), "e_lgs")
                    yield 109
                    dve.wait_ge(s["e_ex"], 1)
                    link(dve, nc.vector.tensor_reduce(mx, lg, AX_X, ALU.add), "e_r")
                    link(dve, nc.vector.reciprocal(mx, mx), "e_r")
                    link(dve, tt(lg, lg, mb, ALU.mult), "e_r")
                    pa = lg.rearrange("p j (e a) -> p j e a", a=1).to_broadcast([128, SEQS, NE, NE])
                    pb = lg.rearrange("p j (a e) -> p j a e", a=1).to_broadcast([128, SEQS, NE, NE])
                    tri = w("before").rearrange("p (a x) -> p a x", a=1).to_broadcast([128, SEQS, NE * NE])
                    fl = lambda x: x.rearrange("p j a b -> p j (a b)")
                    tick(tt(gt, pb, pa, ALU.is_gt), "e_r")
                    link(dve, tt(eq, pb, pa, ALU.is_equal), "e_r")
                    link(dve, tt(fl(eq), fl(eq), tri, ALU.mult), "e_r")
                    link(dve, tt(gt, gt, eq, ALU.add), "e_r")
                    link(dve, nc.vector.tensor_reduce(rank.rearrange("p j (e a) -> p j e a", a=1), gt, AX_X, ALU.add), "e_r")
                    link(dve, stt(rank, rank, 2.0, lg, ALU.is_lt, ALU.mult), "e_r")
                    link(dve, nc.vector.tensor_reduce(mx, rank, AX_X, ALU.add), "e_r")
                    link(dve, ts(mx, mx, 1e-9, None, ALU.add), "e_r")
                    link(dve, nc.vector.reciprocal(mx, mx), "e_r")
                    link(dve, tt(comb, rank, mb, ALU.mult), "e_comb")
                    for e in range(1, NE, 2):
                        yield 113 + e
                        dve.wait_ge(s["e_cb"], e + 1)
                        tick(nc.vector.tensor_copy(side[:, 14 + e], C[:, :]), "e_cd")
                    for e in range(NE):
                        yield 121 + NF * e + 6
                        if e == 0:
                            dve.wait_ge(s["e_ca"], NE // 2)
                        dve.wait_ge(s["e_y"], NF * (e + 1))
                        link(dve, stt(side[:, 9], B[:, :], col(f"eb2_{e}"), side[:, 14 + e], ALU.add, ALU.mult), "e_t")
                        link(dve, tt(h2, h2 if e else h1[:, :], side[:, 9], ALU.add), "e_out" if e == NE - 1 else "e_acc")
                    yield from ln("l_", 1, 200, A, h2, *lnb)
                    for j in range(4):
                        yield 208 + 2 * j
                        dve.wait_ge(s["a_qk"], 2 * j + 2)
                        tick(nc.vector.tensor_copy(side[:, 10 + j], B[:, :]), "a_ke")
                    ms, E, zT = (side[:, 2], side[:, 3]), (side[:, 0], side[:, 1]), side[:, 18:22]
                    four = lambda x: x.rearrange("p (h t) -> p h t", h=4)
                    keep, push = (w(x).rearrange("p (a t) -> p a t", a=1).to_broadcast([128, 4, L]) for x in ("keep", "push"))
                    for i in range(2 * SEQS + 2):
                        mxa, rca, nba, sma = (small[:, a:a + 4].rearrange("p (h a) -> p h a", a=1)
                                              for a in (28, 32, 8 + 4 * (i % 2), 16 + 4 * ((i - 1) % 2)))
                        yield 216 + 3 * i
                        if i < 2 * SEQS:
                            m = ms[i % 2]
                            dve.wait_ge(s["a_s"], i + 1)
                            if i >= 2:
                                dve.wait_ge(s["a_e"], i - 1)
                            link(dve, tt(four(m), four(A[:, :]), keep, ALU.mult), "a_m")
                            link(dve, tt(four(m), four(m), push, ALU.add), "a_ms")
                            link(dve, nc.vector.tensor_reduce(mxa, four(m), AX_X, ALU.max), "a_ms")
                            link(dve, ts(nba, mxa, -0.125, None, ALU.mult), "a_nb")
                        yield 217 + 3 * i
                        if 1 <= i <= 2 * SEQS:
                            dve.wait_ge(s["a_e"], i)
                            if i >= 2:
                                dve.wait_ge(s["a_en"], i - 1)
                            tick(nc.vector.reciprocal(rca, sma), "a_rc")
                        if i >= 2 and i % 2 == 1:
                            j = (i - 2) // 2
                            dve.wait_ge(s["a_z"], i - 1)
                            tick(nc.vector.tensor_copy(zT.rearrange("p a (j t) -> p a j t", j=SEQS)[:, :, j],
                                                       four(C[:, :])), "a_zc")
                    yield 247
                    dve.wait_ge(s["a_o"], 1)
                    link(dve, tt(h3, A[:, :], h2, ALU.add), "a_out")
                    yield from ln("l_", 2, 300, A, h3, *lnb)
                    bits = side[:, 0].bitcast(BF16)
                    yield 306
                    tick(ts(bits[:, 0:T], s_xn, 0.5, None, ALU.is_gt), "f_b")
                    link(dve, ts(bits[:, T:2 * T], s_xn, 0.5, None, ALU.is_ge), "f_b")
                    yield 308
                    first, mor, mand, active = side[:, 14], side[:, 15].bitcast(I32), side[:, 16].bitcast(I32), side[:, 17]
                    dve.wait_ge(s["f_cnt"], 3)
                    tick(stt(first, A[:, :], 0.0, bits[:, 0:T], ALU.is_equal, ALU.mult), "f_mask")
                    tick(ts(mor, B[:, :], 1.0, None, ALU.is_equal), "f_mask")
                    tick(ts(mand, B[:, :], 1.5, None, ALU.is_gt), "f_mask")
                    link(dve, ts(active, C[:, :], 4.5, None, ALU.is_gt), "f_mask")
                    for i in range(1, 8, 2):
                        yield 312 + i
                        m = 128 if i % 4 < 3 else 96
                        dve.wait_ge(s["f_h"], i + 1)
                        tick(ts(side[0:m, 6 + i], C[0:m, :], col(f"lb1_{i % 4}", m), 0.0, ALU.add, ALU.max), "f_rd")
                    yield 322
                    dve.wait_ge(s["f_ye"], 3)
                    ya, yo, yx = side[:, 19], side[:, 20], side[:, 21]
                    link(dve, nc.vector.copy_predicated(yx, mor, yo), "f_s")
                    link(dve, nc.vector.copy_predicated(yx, mand, ya), "f_s")
                    link(dve, ts(yx, yx, 0.0, 15.0, ALU.max, ALU.min), "f_s")
                    link(dve, ts(yx, yx, ROUND, -ROUND, ALU.add, ALU.add), "f_s")
                    link(dve, ts(yx, yx, col("digit"), 2.0, ALU.is_equal, ALU.mult), "f_s")
                    link(dve, tt(yx, yx, active, ALU.mult), "f_s")
                    link(dve, tt(first, h3, s_xn, ALU.add), "f_s")
                    link(dve, tt(first, first, yx, ALU.add), "f_out")

                if do_main:
                    tick(nc.vector.tensor_copy(h_cur[:, :], h_next[:, :]), "m_in")
                    dve.wait_ge(s["m_in"], 1)
                drive(main, token, tail)

            @block.gpsimd
            def _(pool):
                def token():
                    yield TOK0 + 1
                    pool.wait_ge(s["t_rows"], 1)
                    for j in range(SEQS):
                        pool.indirect_dma_start(
                            out=tok[:, 5, j * D:(j + 1) * D], out_offset=None, in_=emb_d,
                            in_offset=bass.IndirectOffsetOnAxis(ap=idx2[:, j:j + 1], axis=0)).then_inc(s[f"t_emb{j}"], 16)
                    yield END - 1
                    for j in range(SEQS):
                        pool.wait_ge(s[f"t_emb{j}"], 16)
                    for j in range(SEQS):
                        pool.dma_reset(range(s[f"t_emb{j}"].num, s[f"t_emb{j}"].num + 1))

                def main():
                    for d in range(2):
                        t0 = 6 + DIR * d
                        yield t0 + 9
                        pool.wait_ge(s["m_lo"], d + 1)
                        tick(nc.gpsimd.tensor_tensor(m_d[:, :, :], m_d[:, :, :], m_e[:, :, :], ALU.mult), "m_low")
                        for st in range(DS):
                            yield t0 + SCAN + 4 * st + 4
                            n = d * DS + st
                            if st == 0:
                                pool.wait_ge(s["m_dtu"], d + 1)
                            pool.wait_ge(s["m_bs"], n + 1)
                            if st >= 2:
                                pool.wait_ge(s["m_scan"], n - 1)
                            b = bs[:, st % 2].rearrange("p (a t) -> p a t", a=1).to_broadcast([128, HALVES, T])
                            tick(nc.gpsimd.tensor_tensor(dbu[st % 2][:, :, :], m_dtu[:, :, :], b, ALU.mult), "m_dbu")

                def tail():
                    E = side[:, 0], side[:, 1]
                    four = lambda x: x.rearrange("p (h t) -> p h t", h=4)
                    rca = small[:, 32:36].rearrange("p (h a) -> p h a", a=1)
                    for i in range(1, 2 * SEQS + 1):
                        yield 217 + 3 * i
                        e = E[(i - 1) % 2]
                        pool.wait_ge(s["a_rc"], i)
                        tick(nc.gpsimd.tensor_tensor(four(e), four(e), rca.to_broadcast([128, 4, L]), ALU.mult), "a_en")

                drive(main, token, tail)

            @block.sync
            def _(sp):
                if do_token:
                    sp.dma_start(idx[:, :], ids_d[:, bass.ds(g_token * SEQS, SEQS)]).then_inc(s["t_ids"], 16)
                if not (do_main or do_tail):
                    sp.wait_ge(s["t_embT"], 1)
                    sp.dma_start(bits_f, bits_d).then_inc(late["bits"], 16)
                    sp.dma_start(W[:, first:NBLOB], blob_d[:, first:NBLOB]).then_inc(late["rest"], 16)
                if do_tail:
                    sp.wait_ge(s["f_osb"], 1)
                    sp.dma_start(out_d[bass.ds(g_out * SEQS, SEQS)].rearrange("j t d -> t j d"),
                                 side[:, 1].rearrange("p (j d) -> p j d", j=SEQS)).then_inc(s["f_done"], 16)
                    sp.wait_ge(s["f_done"], 16)

        numbers = sorted(x.num for x in s.values())
        nc.vector.sem_clear(range(numbers[0], numbers[-1] + 1))
        nc.all_engine_barrier()

    body(0, False, False, 0, True)
    finish()
    body(1, True, False, 0, True)
    if groups > 2:
        with nc.Fori(1, groups - 1) as g:
            body(g + 1, True, True, g - 1, True)
    body(0, True, True, groups - 2, False)
    body(0, False, True, groups - 1, False)
    ctx.close()


def lay_out(x):
    blob = np.zeros((128, NBLOB), np.float32)
    cols = np.zeros((128, len(COLS)), np.float32)
    bits = np.zeros((128, NBITS), np.float32)

    def put(name, a, p0=0, at=0):
        a = a.reshape(a.shape[0], -1)
        blob[p0:p0 + a.shape[0], AT[name][0] + at:AT[name][0] + at + a.shape[1]] = a

    def chunks(a):
        return a.reshape(-1, 128, a.shape[1]).transpose(1, 0, 2).reshape(128, -1)

    def c(name, a):
        cols[0:np.size(a), COL[name]] = a

    put("ident", np.eye(128))
    put("mean", np.full((128, 128), 1 / 128))
    put("headsum", np.kron(np.eye(4), np.ones((32, 32))))
    put("pos", x["L0_tok_pos"][0, 0:L].T)
    for h in range(TH):
        put(f"wqk{h // 4}", x["L0_tok_Wqk"][1][:, h * TDH:(h + 1) * TDH], at=32 * (h % 4))
    for l in range(2):
        put(f"wv{l}", x["L0_tok_Wv"][l])
        put(f"wo{l}", x["L0_tok_Wo"][l])
        put(f"tw1_{l}", x["L0_tok_W1"][l])
        put(f"tw2_{l}", chunks(x["L0_tok_W2"][l]))
        for n, k in (("l1s", "ln1_s"), ("l1b", "ln1_b"), ("l2s", "ln2_s"), ("l2b", "ln2_b"), ("b2", "b2")):
            c(f"t{n}{l}", x["L0_tok_" + k][l])
        for i in range(NF):
            c(f"tb1_{l}{i}", x["L0_tok_b1"][l][128 * i:128 * i + 128])
    c("eps", np.full(128, 1e-5))
    c("one", np.ones(128))
    c("small", np.full(128, 1e-6))
    row16 = (np.arange(128) % 32 == TDH).astype(np.float32)
    c("mask16", row16)
    c("neg16", np.where(row16 > 0, -1.0, 0.0))
    for d in "fb":
        p = f"L0_attn_{d}_"
        put(d + "in", x[p + "in_proj"].T)
        xp, dtw, al, ow = x[p + "x_proj"].T, x[p + "dt_w"].T, x[p + "A_log"], x[p + "out_proj"].T
        put(d + "dtw", dtw)
        put(d + "out", chunks(ow))
        put(d + "alog", chunks(al))
        for h in range(HALVES):
            r = slice(128 * h, 128 * h + 128)
            put(d + "xdt", xp[r, 0:DTR], at=DTR * h)
            for k in range(3):
                put(d + "xbc", xp[r, DTR:DTR + 2 * DS], at=96 * h + 32 * k)
            c(f"{d}w0{h}", x[p + "conv_w"][r, 0, 0])
            c(f"{d}w1{h}", x[p + "conv_w"][r, 0, 1])
            c(f"{d}cb{h}", x[p + "conv_b"][r])
            c(f"{d}dtb{h}", x[p + "dt_b"][r])
            c(f"{d}dsk{h}", x[p + "Dskip"][r])
    put("mw1", x["L0_attn_ffn_w1"].T)
    put("mw2", chunks(x["L0_attn_ffn_w2"].T))
    for i in range(NF):
        c(f"mb1_{i}", x["L0_attn_ffn_b1"][128 * i:128 * i + 128])
    for n, k in (("mb2", "ffn_b2"), ("mg1", "ln1_g"), ("mn1", "ln1_b"), ("mg2", "ln2_g"), ("mn2", "ln2_b")):
        c(n, x["L0_attn_" + k])
    put("router", x["L0_ffn_router_w"])
    put("routerb", np.broadcast_to(x["L0_ffn_router_b"], (128, NE)))
    put("before", np.broadcast_to(np.tril(np.ones((NE, NE)), -1).reshape(1, -1), (128, NE * NE)))
    for e in range(NE):
        put("ew1", x["L0_ffn_w1"][e], at=FF * e)
        put("ew2", chunks(x["L0_ffn_w2"][e]), at=FF * e)
        c(f"eb2_{e}", x["L0_ffn_b2"][e])
        for i in range(NF):
            c(f"eb1_{e}{i}", x["L0_ffn_b1"][e][128 * i:128 * i + 128])
    put("aq", x["L1_attn_W_Q"].reshape(AH * ADH, D).T)
    put("ak", x["L1_attn_W_K"].reshape(AH * ADH, D).T)
    put("av", x["L1_attn_W_V"].reshape(AH * ADH, D).T)
    put("ao", chunks(x["L1_attn_W_O"].T))
    put("keep", np.tril(np.ones((128, 128))))
    put("push", np.where(np.tril(np.ones((128, 128)), -1) > 0, -1e10, 0.0))
    nib, ops = np.zeros((128, 64)), np.zeros((128, 64))
    cum = np.zeros((128, 128))
    for start, operand, row in NIB:
        nib[start:start + 16, 32 * row + operand] = np.arange(16)
        cum[start:start + 16, start:start + 16] = np.triu(np.ones((16, 16)), 1)
    for row in range(2):
        for i, feature in enumerate((2, 3, 1)):
            ops[feature, 32 * row + 2 + i] = 1.0
    put("nibval", nib)
    put("opsel", ops)
    for o, op in enumerate(("and", "or", "xor")):
        p = f"L1_ffn_{op}_"
        w1, w2, b1, b2 = x[p + "w1"], x[p + "w2"][:, RESULT:RESULT + 1], x[p + "b1"], x[p + "b2"]
        for r in range(2):
            for i, feature in enumerate((0, 1, 44, 45, 46)):
                put("lw1", w1[feature:feature + 1, 0:128], p0=32 * r + i, at=128 * o)
                put("lw1", w1[feature:feature + 1, 128:GE], p0=32 * r + i, at=3 * 128 + 32 * o)
            first = (OUT_LO, OUT_HI)[r]
            put("lw2", np.repeat(w2[0:128], 16, axis=1), at=128 * (2 * o + r) + first)
            put("lw2t", np.repeat(w2[128:GE], 16, axis=1), p0=32 * o, at=128 * (2 * o + r) + first)
        c(f"lb1_{o}", b1[0:128])
        cols[32 * o:32 * o + 32, COL["lb1_3"]] = b1[128:GE]
        c(f"lb2_{o}", np.repeat(b2[RESULT:RESULT + 1], 128))
    digit = np.full(128, -1.0)
    digit[OUT_LO:OUT_LO + 16] = digit[OUT_HI:OUT_HI + 16] = np.arange(16)
    c("digit", digit)

    def bit(name, a, at=0):
        bits[0:a.shape[0], BAT[name][0] + at:BAT[name][0] + at + a.shape[1]] = a

    for i in range(2 * DS):
        m = np.zeros((96, 128))
        m[[i, 32 + i, 64 + i]] = 1.0
        bit("bcast", m, at=128 * i)
    bit("fieldcum", cum)
    m = np.zeros((128, 128))
    m[1], m[2] = 2.0, 1.0
    bit("opcode", m)
    m = np.zeros((128, 128))
    m[1:4] = 1.0
    bit("anyop", m)
    m = np.zeros((128, 128))
    m[0] = 4.0
    bit("mark", m)
    return blob, cols, bits


def kernel(**inputs):
    import concourse.bacc as _bacc
    from concourse.bass_utils import run_bass_kernel_spmd as _run

    x = {k: np.asarray(v) for k, v in inputs.items()}
    blob, cols, bits = lay_out(x)
    arrays = {"ids": np.ascontiguousarray(x["x"].T), "emb": np.ascontiguousarray(x["L0_tok_emb"]),
              "blob": blob, "cols": cols, "bits": bits}
    nc = _bacc.Bacc("TRN2", target_bir_lowering=False, num_devices=1)
    args = [nc.dram_tensor(k, a.shape, mybir.dt.from_np(a.dtype), kind="ExternalInput").ap() for k, a in arrays.items()]
    out = nc.dram_tensor("out", (NSEQ, L, D), F32, kind="ExternalOutput").ap()
    build(nc, *args, out)
    r = _run(nc, [arrays], core_ids=[0])
    return r.results[0]["out"]
```
